# Optimizing a Trainium2 kernel written in Bass

```python
import numpy as np
import jax
import jax.numpy as jnp

def _softmax(x, axis=-1):
    return jax.nn.softmax(x, axis=axis)

def _gelu(x):
    return jax.nn.gelu(x, approximate=True)

def _silu(x):
    return jax.nn.silu(x)

def _sigmoid(x):
    return jax.nn.sigmoid(x)

def _layernorm(x, axis=-1, eps=1e-05):
    m = jnp.mean(x, axis=axis, keepdims=True)
    v = jnp.var(x, axis=axis, keepdims=True)
    return (x - m) / jnp.sqrt(v + eps)

def _scatter_add(tgt, idx, src, axis=0):
    return tgt.at[idx].add(src)

def _segment_sum(src, seg, n):
    return jax.ops.segment_sum(src, seg, n)
kernel_name = 'mk_dlrm_tower_d1_rec_r8_2d8ee4'

def setup_inputs(seed: int=0):
    np.random.seed(seed)
    _w = jnp.asarray

    def _rec_inputs():
        import jax
        import jax.numpy as jnp
        _tk = jax.random.key(seed)
        dense_ctx = jax.random.normal(jax.random.fold_in(_tk, 190), (2048, 16), jnp.float32)
        ids = jnp.stack([jax.random.randint(jax.random.fold_in(_tk, 200 + f), (2048,), 0, v, jnp.int32) for f, v in enumerate([12500, 1250, 1250, 125000, 1000, 1250, 12500, 1000, 12500, 125000, 1000, 12500, 1250, 1000, 125000, 1000])], axis=1)
        tbl_0 = 0.05 * jax.random.normal(jax.random.fold_in(_tk, 500 + 0), (12500, 16), jnp.float32)
        tbl_1 = 0.05 * jax.random.normal(jax.random.fold_in(_tk, 500 + 1), (1250, 16), jnp.float32)
        tbl_2 = 0.05 * jax.random.normal(jax.random.fold_in(_tk, 500 + 2), (1250, 16), jnp.float32)
        tbl_3 = 0.05 * jax.random.normal(jax.random.fold_in(_tk, 500 + 3), (125000, 16), jnp.float32)
        tbl_4 = 0.05 * jax.random.normal(jax.random.fold_in(_tk, 500 + 4), (1000, 16), jnp.float32)
        tbl_5 = 0.05 * jax.random.normal(jax.random.fold_in(_tk, 500 + 5), (1250, 16), jnp.float32)
        tbl_6 = 0.05 * jax.random.normal(jax.random.fold_in(_tk, 500 + 6), (12500, 16), jnp.float32)
        tbl_7 = 0.05 * jax.random.normal(jax.random.fold_in(_tk, 500 + 7), (1000, 16), jnp.float32)
        tbl_8 = 0.05 * jax.random.normal(jax.random.fold_in(_tk, 500 + 8), (12500, 16), jnp.float32)
        tbl_9 = 0.05 * jax.random.normal(jax.random.fold_in(_tk, 500 + 9), (125000, 16), jnp.float32)
        tbl_10 = 0.05 * jax.random.normal(jax.random.fold_in(_tk, 500 + 10), (1000, 16), jnp.float32)
        tbl_11 = 0.05 * jax.random.normal(jax.random.fold_in(_tk, 500 + 11), (12500, 16), jnp.float32)
        tbl_12 = 0.05 * jax.random.normal(jax.random.fold_in(_tk, 500 + 12), (1250, 16), jnp.float32)
        tbl_13 = 0.05 * jax.random.normal(jax.random.fold_in(_tk, 500 + 13), (1000, 16), jnp.float32)
        tbl_14 = 0.05 * jax.random.normal(jax.random.fold_in(_tk, 500 + 14), (125000, 16), jnp.float32)
        tbl_15 = 0.05 * jax.random.normal(jax.random.fold_in(_tk, 500 + 15), (1000, 16), jnp.float32)
        _rk = jax.random.fold_in(_tk, 7)
        r_x0 = -0.000233584 + 0.999828 * jax.random.normal(jax.random.fold_in(_rk, 101), (2048, 39, 16), jnp.float32)
        W_top1 = 0.0606339 * jax.random.normal(jax.random.fold_in(_tk, 801), (272, 512), jnp.float32)
        W_top2 = 0.0441942 * jax.random.normal(jax.random.fold_in(_tk, 802), (512, 256), jnp.float32)
        W_top3 = 0.0625 * jax.random.normal(jax.random.fold_in(_tk, 803), (256, 1), jnp.float32)
        b_top1 = jnp.zeros((512,), jnp.float32)
        b_top2 = jnp.zeros((256,), jnp.float32)
        return (dense_ctx, ids, tbl_0, tbl_1, tbl_2, tbl_3, tbl_4, tbl_5, tbl_6, tbl_7, tbl_8, tbl_9, tbl_10, tbl_11, tbl_12, tbl_13, tbl_14, tbl_15, r_x0, W_top1, b_top1, W_top2, b_top2, W_top3)
    dense_ctx, ids, tbl_0, tbl_1, tbl_2, tbl_3, tbl_4, tbl_5, tbl_6, tbl_7, tbl_8, tbl_9, tbl_10, tbl_11, tbl_12, tbl_13, tbl_14, tbl_15, r_x0, W_top1, b_top1, W_top2, b_top2, W_top3 = _rec_inputs()

    def _L0_rec_setup():
        import jax, jax.numpy as jnp
        import numpy as np
        B, S, F, D, K = (1024, 16, 39, 16, 16)
        key = jax.random.key(seed)
        k1, k2, k3, k4, k5 = jax.random.split(key, 5)
        xl = jax.random.normal(k1, (B, S, D), dtype=jnp.float32)
        x0 = jax.random.normal(k2, (B, F, D), dtype=jnp.float32)
        w = jnp.broadcast_to(jnp.eye(D, dtype=jnp.float32), (K, D, D)) + 0.02 * jax.random.normal(k3, (K, D, D), dtype=jnp.float32)
        alpha = jnp.ones((S * F, K), dtype=jnp.float32) + 0.02 * jax.random.normal(k4, (S * F, K), dtype=jnp.float32)
        hv = jnp.ones((K, D, 1), dtype=jnp.float32) + 0.02 * jax.random.normal(k5, (K, D, 1), dtype=jnp.float32)
        return {'xl': xl, 'x0': x0, 'w': w, 'alpha': alpha, 'hv': hv}
    _L0_rec_all = _L0_rec_setup()
    _L0_rec_in = {k: v for k, v in _L0_rec_all.items() if k in ('w', 'alpha', 'hv')}
    del _L0_rec_all
    return {'dense_ctx': dense_ctx, 'ids': ids, 'tbl_0': tbl_0, 'tbl_1': tbl_1, 'tbl_2': tbl_2, 'tbl_3': tbl_3, 'tbl_4': tbl_4, 'tbl_5': tbl_5, 'tbl_6': tbl_6, 'tbl_7': tbl_7, 'tbl_8': tbl_8, 'tbl_9': tbl_9, 'tbl_10': tbl_10, 'tbl_11': tbl_11, 'tbl_12': tbl_12, 'tbl_13': tbl_13, 'tbl_14': tbl_14, 'tbl_15': tbl_15, 'r_x0': r_x0, 'W_top1': W_top1, 'b_top1': b_top1, 'W_top2': W_top2, 'b_top2': b_top2, 'W_top3': W_top3, 'L0_rec_w': _L0_rec_in['w'], 'L0_rec_alpha': _L0_rec_in['alpha'], 'L0_rec_hv': _L0_rec_in['hv']}

def reference(dense_ctx, ids, tbl_0, tbl_1, tbl_2, tbl_3, tbl_4, tbl_5, tbl_6, tbl_7, tbl_8, tbl_9, tbl_10, tbl_11, tbl_12, tbl_13, tbl_14, tbl_15, r_x0, W_top1, b_top1, W_top2, b_top2, W_top3, L0_rec_w, L0_rec_alpha, L0_rec_hv):
    import jax
    import jax.numpy as jnp

    def _L0_rec_ref(xl, x0, w, alpha, hv):
        import jax, jax.numpy as jnp
        import numpy as np
        B, S, F, D, K = (1024, 16, 39, 16, 16)
        b, s, d = xl.shape
        f = x0.shape[1]
        A = jnp.repeat(x0, s, axis=1)
        Bm = jnp.repeat(xl, f, axis=2).reshape(b, s * f, d)
        out = jnp.einsum('bnh,bnd,nk,khd,kd->bkh', A, Bm, alpha, w, hv[..., 0])
        return out
    e = jnp.stack([tbl_0[ids[:, 0]], tbl_1[ids[:, 1]], tbl_2[ids[:, 2]], tbl_3[ids[:, 3]], tbl_4[ids[:, 4]], tbl_5[ids[:, 5]], tbl_6[ids[:, 6]], tbl_7[ids[:, 7]], tbl_8[ids[:, 8]], tbl_9[ids[:, 9]], tbl_10[ids[:, 10]], tbl_11[ids[:, 11]], tbl_12[ids[:, 12]], tbl_13[ids[:, 13]], tbl_14[ids[:, 14]], tbl_15[ids[:, 15]]], axis=1)
    z = _L0_rec_ref(e, r_x0, L0_rec_w, L0_rec_alpha, L0_rec_hv)
    z = z.reshape(z.shape[0], -1)
    h = jnp.concatenate([z, dense_ctx], axis=1)
    h = jnp.maximum(h @ W_top1 + b_top1, 0.0)
    h = jnp.maximum(h @ W_top2 + b_top2, 0.0)
    y = h @ W_top3
    return y

_drawn_inputs = setup_inputs


def setup_inputs(seed=0):
    import zlib

    import numpy as np

    out = dict(_drawn_inputs(seed))
    spreads = {'b_top1': (0.0, 0.1), 'b_top2': (0.0, 0.1)}
    factors = {}
    for name, (base, spread) in spreads.items():
        noise = np.random.default_rng([zlib.crc32(name.encode()), seed]).standard_normal(out[name].shape)
        drawn = base * np.exp(spread * noise) if base else spread * noise
        out[name] = jnp.asarray(drawn.astype(out[name].dtype))
    for name, factor in factors.items():
        out[name] = (out[name] * factor).astype(out[name].dtype)
    return out
```

```python
from contextlib import ExitStack

import concourse.bass as bass
from concourse import mybir

B, F, S, D, K = 2048, 39, 16, 16, 16
P = 128
BT = 4
CH = BT * P
NCH = B // CH
FT = (F + 7) // 8
HP = D // 2
CW = 8
ZW = 2 * K
VOCAB = [12500, 1250, 1250, 125000, 1000, 1250, 12500, 1000, 12500, 125000, 1000, 12500, 1250, 1000, 125000, 1000]
TP = 125
SMALL = [4, 7, 10, 13, 15, 1, 2, 5, 12]
N_FIRST = len(SMALL)
N_LATER = 5
KT = [VOCAB[f] // TP for f in SMALL]
KT_AT = [sum(KT[:n]) for n in range(len(SMALL))]
KT_ALL = sum(KT)
H1, H2 = 512, 256
UNITS = BT * FT * 2
SPAN = 36 // (N_LATER + 1)


def window_start(f):
    base, inner = WINDOWS[f // 8]
    return base + 13 * (f % 8 // 2) + inner * (f % 2)


def _windows():
    found = []
    for ft in range(FT):
        fs = range(8 * ft, min(8 * ft + 8, F))
        found.append(next((base, inner) for base in range(S * D) for inner in range(4, 9)
                          if all(0 <= 256 * f // F - (base + 13 * (f % 8 // 2) + inner * (f % 2))
                                 and (256 * f + 255) // F - (base + 13 * (f % 8 // 2) + inner * (f % 2)) < CW
                                 for f in fs)))
    return found


WINDOWS = _windows()
EC = max(window_start(f) for f in range(8 * FT)) + CW


def program(nc, t):
    fp32, bf16, fp16, i32 = mybir.dt.float32, mybir.dt.bfloat16, mybir.dt.float16, mybir.dt.int32
    ALU, ACT, AX = mybir.AluOpType, mybir.ActivationFunctionType, mybir.AxisListType
    gathered_first = [f for f in range(S) if f not in SMALL[:N_FIRST]]
    gathered_later = [f for f in range(S) if f not in SMALL[:N_LATER]]

    ctx = ExitStack()
    with ctx:
        def sb(name, shape, dt):
            return ctx.enter_context(nc.sbuf_tensor(name, shape, dt))

        def sem(name):
            return ctx.enter_context(nc.semaphore(name))

        banks = [ctx.enter_context(nc.psum_tensor(f"bank{n}", [P, 512], fp32)) for n in range(8)]
        x_bank, z_bank, o_bank, w_bank = banks[0:2], banks[2:4], banks[4:6], banks[6:8]

        ident = sb("ident", [P, P], fp32)
        tower = sb("tower", [P, 10 * CH], fp32)
        h1 = tower[:, 0:4 * CH].rearrange("p (a c) -> p a c", a=H1 // P)
        h2 = tower[:, 4 * CH:6 * CH].rearrange("p (a c) -> p a c", a=H2 // P)
        z_t = tower[:, 6 * CH:8 * CH].rearrange("p (a c) -> p a c", a=2)
        z = tower[:, 8 * CH:10 * CH].rearrange("p (a c) -> p a c", a=BT)
        windows_c = tower[:].rearrange("p (g d c) -> p g d c", g=FT, d=D)
        h_mask = sb("h_mask", [P, 2 * P], fp32)
        k_mask = sb("k_mask", [P, K], fp32)
        row_no = sb("row_no", [P, KT_ALL], fp32)
        alpha = sb("alpha", [P, FT, K], fp32)
        w_dk = sb("w_dk", [P, 2, D], fp32)
        hv_dk = sb("hv_dk", [P, 2, 1], fp32)
        v_dk = sb("v_dk", [P, 2, D], fp32)
        v_diag = sb("v_diag", [P, 2, 2 * P], fp32)
        ab = sb("ab", [P // 2, FT, 2 * P], fp32)
        ab_t = sb("ab_t", [P, FT, 2, P], fp32)
        m_w = sb("m_w", [P, FT, 2 * P], fp32)
        table = sb("table", [TP, KT_ALL, D], fp32)
        rest1 = sb("rest1", [TP, KT_ALL, D], fp32)
        rest2 = sb("rest2", [TP, KT_ALL, D], fp32)
        parts = sb("parts", [TP, KT_ALL, 3, D], bf16)
        ids_all = sb("ids_all", [P, B // P, S], i32)
        ids_now = sb("ids_now", [P, BT, S], i32)
        ids_flat = sb("ids_flat", [P, S * B // P], i32)
        ids_half = sb("ids_half", [P, S * B // P], fp16)
        ids_b = sb("ids_b", [TP, N_LATER, B], fp16)
        ids_b0 = sb("ids_b0", [TP, N_FIRST - N_LATER, CH], fp16)
        onehot = sb("onehot", [TP, 2, max(KT), CH], bf16)
        e = sb("e", [P, BT, EC], fp32)
        e_cols = sb("e_cols", [P, BT, FT * P], fp32)
        e_win = sb("e_win", [P, FT, CH], fp32)
        x0 = sb("x0", [P, 2, CW, FT * P], fp32)
        prod = sb("prod", [P, 2, 512], fp32)
        ctx_t = sb("ctx_t", [D, B], fp32)
        w1_z = sb("w1_z", [P, 2, H1], fp32)
        w1_c = sb("w1_c", [D, H1], fp32)
        w2 = sb("w2", [P, H1 // P, H2], fp32)
        w3 = sb("w3", [P, H2 // P, 1], fp32)
        b1 = sb("b1", [P, H1 // P], fp32)
        b2 = sb("b2", [P, H2 // P], fp32)
        y = sb("y", [P, B // P], fp32)
        y_rows = sb("y_rows", [B // P, P], fp32)

        in_ids = sem("in_ids")
        in_ids_flat = sem("in_ids_flat")
        ids_stored = sem("ids_stored")
        in_ids_b = sem("in_ids_b")
        in_small = sem("in_small")
        in_win = sem("in_win")
        in_tables = sem("in_tables")
        in_tower = sem("in_tower")
        in_x0 = [sem(f"in_x0_{slot}") for slot in range(2)]
        gathered = sem("gathered")
        out_stored = sem("out_stored")
        ids_cast = sem("ids_cast")
        padded = sem("padded")
        v_made = sem("v_made")
        v_spread = sem("v_spread")
        ab_summed = sem("ab_summed")
        ab_kept = sem("ab_kept")
        ab_turned = sem("ab_turned")
        ab_t_kept = sem("ab_t_kept")
        m_summed = sem("m_summed")
        m_kept = sem("m_kept")
        split = sem("split")
        rest_made = sem("rest_made")
        ids_copied = sem("ids_copied")
        gathers_begun = sem("gathers_begun")
        hot_made = sem("hot_made")
        hot_used = sem("hot_used")
        rows_kept = sem("rows_kept")
        e_spread = sem("e_spread")
        win_turned = sem("win_turned")
        win_kept = sem("win_kept")
        x_turned = sem("x_turned")
        prod_made = sem("prod_made")
        z_summed = sem("z_summed")
        z_kept = sem("z_kept")
        z_turned = sem("z_turned")
        z_t_kept = sem("z_t_kept")
        h1_summed = sem("h1_summed")
        h1_made = sem("h1_made")
        h2_summed = sem("h2_summed")
        h2_made = sem("h2_made")
        y_summed = sem("y_summed")
        w0_free = sem("w0_free")
        y_turned = sem("y_turned")
        y_kept = sem("y_kept")

        N_SMALL_LOADS = 7
        N_TOWER_LOADS = 7

        def tables_before(chunk):
            return chunk * N_LATER + (N_FIRST - N_LATER)

        def gathers_through(chunk):
            return chunk * (BT * len(gathered_later)) + BT * len(gathered_first)

        block = ctx.enter_context(nc.Block())

        @block.sync
        def _(sp):
            sp.dma_start(ids_flat[:], t["ids_t"].rearrange("f (a b) -> (f a) b", b=S * B // P)).then_inc(in_ids_flat, 16)
            sp.dma_start(ids_all[:], t["ids"].rearrange("(t p) f -> p t f", p=P)).then_inc(in_ids, 16)
            sp.dma_start(row_no[:], t["row_no"]).then_inc(in_small, 16)
            sp.dma_start(ident[:], t["ident"]).then_inc(in_small, 16)
            sp.dma_start(k_mask[:], t["k_mask"]).then_inc(in_small, 16)
            sp.dma_start(h_mask[:], t["h_mask"]).then_inc(in_small, 16)
            sp.dma_start(w_dk[:], t["w_dk"].rearrange("(a p) h -> p a h", p=P)).then_inc(in_small, 16)
            sp.dma_start(hv_dk[:, :, 0], t["hv_dk"]).then_inc(in_small, 16)
            sp.dma_start(alpha[:], t["alpha"].rearrange("(g p) k -> p g k", p=P)).then_inc(in_small, 16)
            sp.dma_start(windows_c, t["windows_c"]).then_inc(in_win, 16)
            sp.wait_ge(ids_stored, 16)
            for n in range(N_FIRST):
                row = t["ids_half"][SMALL[n]:SMALL[n] + 1, :]
                if n < N_LATER:
                    sp.dma_start(ids_b[:, n, :], row.to_broadcast([TP, B])).then_inc(in_ids_b, 16)
                else:
                    sp.dma_start(ids_b0[:, n - N_LATER, :], row[:, 0:CH].to_broadcast([TP, CH])).then_inc(in_ids_b, 16)
            def load_x0(rows, slot):
                sp.dma_start(x0[:, slot, :, :], t["x0"][rows, :].unsqueeze(1).to_broadcast([P, CW, FT * P])
                             ).then_inc(in_x0[slot], 16)

            for bt in range(2):
                load_x0(bass.ds(bt * P, P), bt)
            sp.dma_start(w1_z[:], t["w1_z"].rearrange("(a p) n -> p a n", p=P)).then_inc(in_tower, 16)
            sp.dma_start(w1_c[:], t["w1_c"]).then_inc(in_tower, 16)
            sp.dma_start(ctx_t[:], t["ctx_t"]).then_inc(in_tower, 16)
            sp.dma_start(b1[:], t["b1"]).then_inc(in_tower, 16)
            sp.dma_start(w2[:], t["w2"].rearrange("(a p) n -> p a n", p=P)).then_inc(in_tower, 16)
            sp.dma_start(b2[:], t["b2"]).then_inc(in_tower, 16)
            sp.dma_start(w3[:, :, 0], t["w3"]).then_inc(in_tower, 16)

            def reload_x0(i, bt):
                sp.wait_ge(x_turned, i * UNITS + (bt + 1) * (UNITS // BT))
                load_x0(bass.ds(i * CH + (bt + 2) * P, P), bt % 2)

            with sp.Fori(0, NCH - 1) as i:
                for bt in range(BT):
                    reload_x0(i, bt)
            for bt in range(BT - 2):
                reload_x0(NCH - 1, bt)

        @block.gpsimd
        def _(pool):
            def gathers(fields):
                for bt in range(BT):
                    for f in fields:
                        nc.gpsimd.indirect_dma_start(
                            out=e[:, bt, f * D:(f + 1) * D], out_offset=None, in_=t[f"tbl_{f}"][:, :],
                            in_offset=bass.IndirectOffsetOnAxis(ap=ids_now[:, bt, f:f + 1], axis=0)).then_inc(gathered, 16)

            pool.wait_ge(in_ids, 16)
            nc.gpsimd.tensor_copy(ids_now[:], ids_all[:, 0:BT, :]).then_inc(ids_copied, 1)
            pool.wait_ge(ids_copied, 1)
            gathers(gathered_first)
            with pool.Fori(1, NCH) as c:
                pool.wait_ge(e_spread, c)
                pool.sem_inc(gathers_begun, 1)
                nc.gpsimd.tensor_copy(ids_now[:], ids_all[:, bass.ds(c * BT, BT), :]).then_inc(ids_copied, 1)
                pool.wait_ge(ids_copied, c + 1)
                pool.sem_inc(gathers_begun, 1)
                gathers(gathered_later)

        @block.vector
        def _(dve):
            def make_hot(n, first_slot, slots, chunk):
                for k in range(first_slot, first_slot + slots):
                    if chunk is None:
                        ids = ids_b[:, n, 0:CH] if n < N_LATER else ids_b0[:, n - N_LATER, :]
                    else:
                        ids = ids_b[:, n, bass.ds(chunk * CH, CH)]
                    last = nc.vector.tensor_scalar(onehot[:, n % 2, k, :], ids, row_no[0:TP, KT_AT[n] + k:KT_AT[n] + k + 1],
                                                   None, ALU.is_equal)
                if first_slot + slots == KT[n]:
                    last.then_inc(hot_made, 1)

            def keep_rows(n):
                parts_ps = o_bank[n % 2][:, 0:BT * 3 * D].rearrange("p (b s d) -> p b d s", b=BT, s=3)
                f = SMALL[n]
                nc.vector.tensor_reduce(e[:, :, f * D:(f + 1) * D], parts_ps, AX.X, ALU.add).then_inc(rows_kept, 1)

            def keep_windows(chunk):
                for ft in range(FT):
                    dve.wait_ge(win_turned, chunk * FT + ft + 1)
                    nc.vector.tensor_copy(e_win[:, ft, :], o_bank[ft % 2][:]).then_inc(win_kept, 1)

            dve.wait_ge(in_ids_flat, 16)
            nc.vector.tensor_scalar(ids_half[:], ids_flat[:], 2048.0, None, ALU.min).then_inc(ids_cast, 1)
            nc.vector.memset(e[:, :, S * D:], 0.0).then_inc(padded, 1)
            dve.wait_ge(in_small, 16 * N_SMALL_LOADS)
            for a in range(2):
                last = nc.vector.tensor_scalar(v_dk[:, a, :], w_dk[:, a, :], hv_dk[:, a, :], None, ALU.mult)
            last.then_inc(v_made, 1)
            dve.wait_ge(v_made, 1)
            for a in range(2):
                last = nc.vector.tensor_tensor(
                    v_diag[:, a, :].rearrange("p (g k h) -> p g k h", g=HP, k=K),
                    v_dk[:, a, :].rearrange("p (g h) -> p g h", g=HP).unsqueeze(2).to_broadcast([P, HP, K, 2]),
                    k_mask[:].unsqueeze(1).unsqueeze(3).to_broadcast([P, HP, K, 2]), ALU.mult)
            last.then_inc(v_spread, 1)
            for ft in range(0, FT, 2):
                n = min(2, FT - ft)
                dve.wait_ge(ab_summed, ft // 2 + 1)
                src = (w_bank + z_bank)[ft // 2][0:P // 2, 0:n * 2 * P]
                nc.vector.tensor_copy(ab[:, ft:ft + n, :].rearrange("p a c -> p (a c)"), src).then_inc(ab_kept, 1)
            dve.wait_ge(split, 1)
            nc.vector.tensor_tensor(rest1[:], table[:], parts[:, :, 0, :], ALU.subtract).then_inc(rest_made, 1)
            dve.wait_ge(in_ids_b, 16 * N_FIRST)
            make_hot(0, 0, KT[0], None)
            dve.wait_ge(split, 2)
            nc.vector.tensor_tensor(rest2[:], rest1[:], parts[:, :, 1, :], ALU.subtract).then_inc(rest_made, 1)
            make_hot(1, 0, KT[1], None)
            for ft in range(0, FT, 2):
                n = min(2, FT - ft)
                dve.wait_ge(m_summed, ft // 2 + 1)
                src = (w_bank + z_bank)[ft // 2][:, 0:n * 2 * P].rearrange("p (a c) -> p a c", a=n)
                last = nc.vector.tensor_tensor(m_w[:, ft:ft + n, :], src,
                                               h_mask[:].unsqueeze(1).to_broadcast([P, n, 2 * P]), ALU.mult)
                last.then_inc(m_kept, 1)
            nc.vector.memset(y[:, 0:1], 0.0).then_inc(w0_free, 1)
            for n in range(N_FIRST):
                dve.wait_ge(hot_used, n + 1)
                keep_rows(n)
                if n + 2 < N_FIRST:
                    make_hot(n + 2, 0, KT[n + 2], None)
            keep_windows(0)

            def chunk_units(i, more):
                for u in range(UNITS):
                    bt, ft = u // (2 * FT), u % (2 * FT) // 2
                    dve.wait_ge(x_turned, i * UNITS + u + 1)
                    if u >= 2:
                        dve.wait_ge(z_summed, i * UNITS + u - 1)
                    elif u == 0:
                        dve.wait_ge(win_kept, (i + 1) * FT)
                    nc.vector.tensor_tensor(
                        prod[:, u % 2, :].rearrange("p (q b) -> p q b", q=4),
                        x_bank[u % 2][:].rearrange("p (q b) -> p q b", q=4),
                        e_win[:, ft, bt * P:(bt + 1) * P].unsqueeze(1).to_broadcast([P, 4, P]),
                        ALU.mult).then_inc(prod_made, 1)
                    if not more:
                        continue
                    base = tables_before(i + 1)
                    n, at = u // SPAN, u % SPAN
                    if n < N_LATER:
                        if at == 0:
                            dve.wait_ge(hot_used, base + max(n - 1, 0))
                        lo, hi = KT[n] * at // SPAN, KT[n] * (at + 1) // SPAN
                        if hi > lo:
                            make_hot(n, lo, hi - lo, i + 1)
                    n, at = u // SPAN - 2, u % SPAN
                    if 0 <= n < N_LATER and at == 1:
                        dve.wait_ge(hot_used, base + n + 1)
                        keep_rows(n)
                if more:
                    dve.wait_ge(prod_made, (i + 1) * UNITS)
                    keep_windows(i + 1)

            with dve.Fori(0, NCH - 1) as i:
                chunk_units(i, True)
            chunk_units(NCH - 1, False)

        @block.scalar
        def _(act):
            for n in range(N_FIRST):
                act.dma_start(table[:, KT_AT[n]:KT_AT[n] + KT[n], :],
                              t[f"tbl_{SMALL[n]}"].rearrange("(p k) d -> p k d", p=TP)).then_inc(in_tables, 16)
            act.wait_ge(ids_cast, 1)
            act.dma_start(t["ids_half"].rearrange("f (a b) -> (f a) b", b=S * B // P), ids_half[:]).then_inc(ids_stored, 16)
            act.wait_ge(in_tables, 16 * N_FIRST)
            nc.scalar.copy(parts[:, :, 0, :], table[:]).then_inc(split, 1)
            act.wait_ge(rest_made, 1)
            nc.scalar.copy(parts[:, :, 1, :], rest1[:]).then_inc(split, 1)
            for ft in range(0, FT, 2):
                n = min(2, FT - ft)
                act.wait_ge(ab_turned, ft // 2 + 1)
                src = (x_bank + z_bank[1:])[ft // 2][:, 0:n * P].unsqueeze(2).to_broadcast([P, n * P, 2])
                nc.scalar.copy(ab_t[:, ft:ft + n, :, :].rearrange("p a s (c h) -> p (a s c) h", h=2), src).then_inc(ab_t_kept, 1)
            act.wait_ge(rest_made, 2)
            nc.scalar.copy(parts[:, :, 2, :], rest2[:]).then_inc(split, 1)

            def spread_e(chunk, tables, chunk_is_first):
                act.wait_ge(rows_kept, tables)
                act.wait_ge(gathered, gathers_through(chunk) * 16)
                if not chunk_is_first:
                    act.wait_ge(win_turned, chunk * FT)
                else:
                    act.wait_ge(padded, 1)
                for ft in range(FT):
                    base, inner = WINDOWS[ft]
                    for fi in range(4):
                        f_lo, h = divmod(fi, 2)
                        src = bass.AP(e, base + inner * f_lo, [[BT * EC, P], [EC, BT], [1, CW], [13, 4]])
                        dst = bass.AP(e_cols, ft * P + 2 * f_lo + h, [[BT * FT * P, P], [FT * P, BT], [16, CW], [4, 4]])
                        last = nc.scalar.copy(dst, src)
                last.then_inc(e_spread, 1)

            spread_e(0, N_FIRST, True)
            act.wait_ge(in_tower, 16 * N_TOWER_LOADS)

            def chunk_tower(i, more):
                for half in range(2):
                    if half == 1 and more:
                        spread_e(i + 1, tables_before(i + 2), False)
                    act.wait_ge(z_summed, i * UNITS + (half + 1) * (UNITS // 2))
                    nc.scalar.copy(z[:, 2 * half:2 * half + 2, :].rearrange("p a c -> p (a c)"),
                                   z_bank[half][:]).then_inc(z_kept, 1)
                act.wait_ge(z_turned, i + 1)
                for a in range(2):
                    nc.scalar.copy(z_t[:, a, :], w_bank[a][:]).then_inc(z_t_kept, 1)
                for m in range(H1 // P):
                    act.wait_ge(h1_summed, i * (H1 // P) + m + 1)
                    nc.scalar.activation(h1[:, m, :], w_bank[m % 2][:], ACT.Relu, bias=b1[:, m:m + 1]).then_inc(h1_made, 1)
                for n in range(H2 // P):
                    act.wait_ge(h2_summed, i * (H2 // P) + n + 1)
                    nc.scalar.activation(h2[:, n, :], w_bank[n % 2][:], ACT.Relu, bias=b2[:, n:n + 1]).then_inc(h2_made, 1)
                act.wait_ge(y_summed, i + 1)
                nc.scalar.copy(y[:, bass.ds(i * BT, BT)], w_bank[0][:, 0:BT]).then_inc(w0_free, 1)

            with act.Fori(0, NCH - 1) as i:
                chunk_tower(i, True)
            chunk_tower(NCH - 1, False)
            act.wait_ge(y_turned, 1)
            nc.scalar.copy(y_rows[:], w_bank[1][0:B // P, 0:P]).then_inc(y_kept, 1)
            act.wait_ge(y_kept, 1)
            act.dma_start(t["out"].rearrange("(t p) o -> t (p o)", p=P), y_rows[:]).then_inc(out_stored, 16)
            act.wait_ge(out_stored, 16)

        @block.tensor
        def _(pe):
            def table_rows(n, k0, k1):
                for k in range(k0, k1):
                    bt, slot = divmod(k, KT[n])
                    last = nc.tensor.matmul(o_bank[n % 2][:, bt * 3 * D:(bt + 1) * 3 * D],
                                            onehot[:, n % 2, slot, bt * P:(bt + 1) * P],
                                            parts[:, KT_AT[n] + slot, :, :].rearrange("p s d -> p (s d)"),
                                            start=slot == 0, stop=slot == KT[n] - 1)
                if k1 == BT * KT[n]:
                    last.then_inc(hot_used, 1)

            def turn_windows(ft):
                for bt in range(BT):
                    last = nc.tensor.transpose(o_bank[ft % 2][:, bt * P:(bt + 1) * P],
                                               e_cols[:, bt, ft * P:(ft + 1) * P], ident[:])
                last.then_inc(win_turned, 1)

            def turn_x(u):
                bt, ft, half = u // (2 * FT), u % (2 * FT) // 2, u % 2
                row = CW * FT * P
                for q in range(4):
                    at = (bt % 2) * row + ft * HP + 4 * half + q
                    src = bass.AP(x0, at, [[2 * row, P], [FT * HP, P]])
                    last = nc.tensor.transpose(x_bank[u % 2][:, q * P:(q + 1) * P], src, ident[:])
                last.then_inc(x_turned, 1)

            def contract(u):
                bt, ft, half = u // (2 * FT), u % (2 * FT) // 2, u % 2
                for q in range(4):
                    hp = 4 * half + q
                    at = (bt % 2) * 2 * P + hp * ZW
                    last = nc.tensor.matmul(z_bank[bt // 2][:, at:at + ZW], prod[:, u % 2, q * P:(q + 1) * P],
                                            m_w[:, ft, hp * ZW:(hp + 1) * ZW],
                                            start=ft == 0 and hp == 0, stop=ft == FT - 1, skip_group_check=True)
                last.then_inc(z_summed, 1)

            def turn_z(half):
                for bt in (2 * half, 2 * half + 1):
                    for a in range(2):
                        last = nc.tensor.transpose(w_bank[a][:, bt * P:(bt + 1) * P], z[:, bt, a * P:(a + 1) * P], ident[:])
                return last

            pe.wait_ge(in_small, 16 * N_SMALL_LOADS)
            pe.wait_ge(in_win, 16)
            ab_bank = w_bank + z_bank
            for ft in range(FT):
                for d in range(D):
                    at = (ft % 2) * 2 * P + d * K
                    last = nc.tensor.matmul(ab_bank[ft // 2][0:P // 2, at:at + K], windows_c[:, ft, d, :], alpha[:, ft, :], start=True, stop=True)
                if ft % 2 or ft == FT - 1:
                    last.then_inc(ab_summed, 1)
            turned_bank = x_bank + z_bank[1:]
            for ft in range(FT):
                if ft % 2 == 0:
                    pe.wait_ge(ab_kept, ft // 2 + 1)
                for a in range(2):
                    at = (ft % 2 * 2 + a) * (P // 2)
                    last = nc.tensor.transpose(turned_bank[ft // 2][:, at:at + P // 2], ab[:, ft, a * P:(a + 1) * P],
                                               ident[0:P // 2, 0:P // 2])
                if ft % 2 or ft == FT - 1:
                    last.then_inc(ab_turned, 1)
            pe.wait_ge(v_spread, 1)
            for ft in range(FT):
                if ft % 2 == 0:
                    pe.wait_ge(ab_t_kept, ft // 2 + 1)
                at = ft % 2 * 2 * P
                for a in range(2):
                    last = nc.tensor.matmul(ab_bank[ft // 2][:, at:at + 2 * P], ab_t[:, ft, a, :], v_diag[:, a, :],
                                            start=a == 0, stop=a == 1)
                if ft % 2 or ft == FT - 1:
                    last.then_inc(m_summed, 1)
            pe.wait_ge(in_x0[0], 16)
            for u in range(2):
                turn_x(u)
            pe.wait_ge(split, 3)
            for n in range(N_FIRST):
                pe.wait_ge(hot_made, n + 1)
                if n >= 2:
                    pe.wait_ge(rows_kept, n - 1)
                table_rows(n, 0, BT * KT[n])
            pe.wait_ge(e_spread, 1)
            for ft in range(FT):
                if ft >= 2:
                    pe.wait_ge(win_kept, ft - 1)
                turn_windows(ft)
            pe.wait_ge(m_kept, (FT + 1) // 2)
            pe.wait_ge(in_tower, 16 * N_TOWER_LOADS)

            def chunk_all(i, more):
                for u in range(UNITS):
                    pe.wait_ge(prod_made, i * UNITS + u + 1)
                    contract(u)
                    if u + 2 < UNITS:
                        if (u + 2) % (UNITS // BT) == 0:
                            bt = (u + 2) // (UNITS // BT)
                            pe.wait_ge(in_x0[bt % 2], i * 32 + 16 * (bt // 2 + 1))
                        turn_x(u + 2)
                    if more:
                        base = tables_before(i + 1)
                        n, at = u // SPAN - 1, u % SPAN
                        if 0 <= n < N_LATER:
                            if at == 0:
                                pe.wait_ge(hot_made, base + n + 1)
                                if n == 0:
                                    pe.wait_ge(win_kept, (i + 1) * FT)
                                if n >= 2:
                                    pe.wait_ge(rows_kept, base + n - 1)
                            table_rows(n, BT * KT[n] * at // SPAN, BT * KT[n] * (at + 1) // SPAN)
                    if u == UNITS // 2 + 2:
                        pe.wait_ge(z_kept, i * 2 + 1)
                        pe.wait_ge(w0_free, i + 1)
                        turn_z(0)
                if more:
                    pe.wait_ge(in_x0[0], i * 32 + 48)
                    for u in range(2):
                        turn_x(u)
                pe.wait_ge(z_kept, i * 2 + 2)
                turn_z(1).then_inc(z_turned, 1)
                if more:
                    pe.wait_ge(e_spread, i + 2)
                    turn_windows(0)
                    turn_windows(1)

                def window_step(ft):
                    if more:
                        pe.wait_ge(win_kept, (i + 1) * FT + ft - 1)
                        turn_windows(ft)

                pe.wait_ge(z_t_kept, i * 2 + 2)
                for m in range(H1 // P):
                    if m >= 2:
                        pe.wait_ge(h1_made, i * (H1 // P) + m - 1)
                    for a in range(2):
                        nc.tensor.matmul(w_bank[m % 2][:], w1_z[:, a, m * P:(m + 1) * P], z_t[:, a, :],
                                         start=a == 0, stop=False)
                    nc.tensor.matmul(w_bank[m % 2][:], w1_c[:, m * P:(m + 1) * P], ctx_t[:, bass.ds(i * CH, CH)],
                                     start=False, stop=True).then_inc(h1_summed, 1)
                    if m == 1:
                        window_step(2)
                window_step(3)
                for n in range(H2 // P):
                    for m in range(H1 // P):
                        if n == 0 and m >= 2:
                            pe.wait_ge(h1_made, i * (H1 // P) + m + 1)
                        if n == 0 and m == 0:
                            pe.wait_ge(h1_made, i * (H1 // P) + 3)
                        last = nc.tensor.matmul(w_bank[n % 2][:], w2[:, m, n * P:(n + 1) * P], h1[:, m, :],
                                                start=m == 0, stop=m == H1 // P - 1)
                    last.then_inc(h2_summed, 1)
                window_step(4)
                pe.wait_ge(h2_made, (i + 1) * (H2 // P))
                for bt in range(BT):
                    for n in range(H2 // P):
                        last = nc.tensor.matmul(w_bank[0][:, bt:bt + 1], h2[:, n, bt * P:(bt + 1) * P], w3[:, n, :],
                                                start=n == 0, stop=n == H2 // P - 1)
                last.then_inc(y_summed, 1)

            with pe.Fori(0, NCH - 1) as i:
                chunk_all(i, True)
            chunk_all(NCH - 1, False)
            pe.wait_ge(w0_free, NCH + 1)
            nc.tensor.transpose(w_bank[1][0:B // P, 0:P], y[:], ident[:]).then_inc(y_turned, 1)


def _constants():
    import numpy as np
    part = np.arange(P)
    windows_c = np.zeros((P, FT, D, CW, 8), np.float32)
    for f in range(F):
        for g in range(256):
            j, d = divmod(g, D)
            windows_c[(f % 8) * 16 + j, f // 8, d, (256 * f + g) // F - window_start(f), f % 8] = 1.0
    h_mask = (part[:, None] % 2 == np.arange(2 * P)[None, :] % 2).astype(np.float32)
    k_mask = (part[:, None] % K == np.arange(K)[None, :]).astype(np.float32)
    row_no = np.concatenate([part[:, None] * kt + np.arange(kt)[None, :] for kt in KT], axis=1).astype(np.float32)
    return {"windows_c": windows_c.reshape(P, FT, D, 64), "h_mask": h_mask, "k_mask": k_mask,
            "row_no": row_no, "ident": np.eye(P, dtype=np.float32)}


def kernel(**inputs):
    import numpy as np
    import concourse.bacc as bacc
    from concourse.bass_utils import run_bass_kernel_spmd

    a = {name: np.asarray(value) for name, value in inputs.items()}
    w1 = a["W_top1"]
    x0 = np.concatenate([a["r_x0"], np.zeros((B, 8 * FT - F, D), np.float32)], axis=1)
    x0 = x0.reshape(B, FT, 8, HP, 2).transpose(0, 2, 4, 1, 3)
    arrays = _constants()
    arrays.update({f"tbl_{f}": a[f"tbl_{f}"] for f in range(S)})
    arrays.update({
        "ids": a["ids"], "ids_t": a["ids"].T, "x0": x0.reshape(B, FT * P), "ctx_t": a["dense_ctx"].T,
        "alpha": np.concatenate([a["L0_rec_alpha"], np.zeros((8 * 16 * FT - S * F, K), np.float32)]),
        "w_dk": a["L0_rec_w"].transpose(2, 0, 1).reshape(D * K, D),
        "hv_dk": a["L0_rec_hv"].transpose(1, 0, 2).reshape(2, P).T,
        "w1_z": w1[0:K * D].reshape(K, HP, 2, H1).transpose(1, 0, 2, 3).reshape(K * D, H1), "w1_c": w1[K * D:],
        "b1": a["b_top1"].reshape(H1 // P, P).T, "w2": a["W_top2"], "b2": a["b_top2"].reshape(H2 // P, P).T,
        "w3": a["W_top3"].reshape(H2 // P, P).T,
    })
    arrays = {f"{name}_dram": np.ascontiguousarray(value) for name, value in arrays.items()}

    nc = bacc.Bacc("TRN2", target_bir_lowering=False, num_devices=1)
    t = {name.removesuffix("_dram"): nc.dram_tensor(name, value.shape, mybir.dt.from_np(value.dtype), kind="ExternalInput").ap()
         for name, value in arrays.items()}
    t["ids_half"] = nc.dram_tensor("ids_half_dram", (S, B), mybir.dt.float16).ap()
    t["out"] = nc.dram_tensor("out_dram", (B, 1), mybir.dt.float32, kind="ExternalOutput").ap()
    program(nc, t)
    return run_bass_kernel_spmd(nc, [arrays], core_ids=[0]).results[0]["out_dram"]
```

```python
from contextlib import ExitStack

import concourse.bass as bass
from concourse import mybir

B, F, S, D, K = 2048, 39, 16, 16, 16
P = 128
BT = 4
CH = BT * P
NCH = B // CH
FT = (F + 7) // 8
HP = D // 2
QH = HP // 2
UNITS = 2 * FT
CW = 8
ZW = 2 * K
X_SLOTS = 5
VOCAB = [12500, 1250, 1250, 125000, 1000, 1250, 12500, 1000, 12500, 125000, 1000, 12500, 1250, 1000, 125000, 1000]
TP = 125
NEW = [[0, 1, 2, 3], [4, 5, 6], [7, 8, 9], [10, 11, 12, 13], [14, 15]]
HOT_FIRST = [[1, 2], [4, 5], [7], [10, 12, 13], [15]]
HOT_LATER = [[1], [4], [7], [10], [15]]
HOT = sum(HOT_LATER, []) + [f for f in sum(HOT_FIRST, []) if f not in sum(HOT_LATER, [])]
N_LATER = len(HOT_LATER)
N_HOT = len(HOT)
KT = {f: VOCAB[f] // TP for f in HOT}
KT_AT = {f: sum(KT[g] for g in HOT[:n]) for n, f in enumerate(HOT)}
KT_ALL = sum(KT.values())
H1, H2 = 512, 256


def _windows():
    found = []
    for ft in range(FT):
        fs = range(8 * ft, min(8 * ft + 8, F))
        found.append(next((base, inner) for base in range(S * D) for inner in range(4, 9)
                          if all(0 <= 256 * f // F - (base + 13 * (f % 8 // 2) + inner * (f % 2))
                                 and (256 * f + 255) // F - (base + 13 * (f % 8 // 2) + inner * (f % 2)) < CW
                                 for f in fs)))
    return found


WINDOWS = _windows()


def window_start(f):
    base, inner = WINDOWS[f // 8]
    return base + 13 * (f % 8 // 2) + inner * (f % 2)


EC = max(window_start(f) for f in range(8 * FT)) + CW

TABLES_0 = {-1: [(0, 0), (0, 1)], 0: [(0, 2)], 1: [(1, 0)], 2: [(0, 3)], 3: [(1, 1)], 4: [(0, 4)], 5: [(1, 2)],
            7: [(1, 3)], 9: [(1, 4)]}
WINS_0 = {-1: [(0, 0)], 0: [(0, 1)], 2: [(0, 2)], 4: [(0, 3)], 5: [(1, 0)], 6: [(0, 4)], 7: [(1, 1)], 9: [(1, 2)],
          10: [(1, 3)], 11: [(1, 4)]}
TABLES_N = {1: [(1, 0)], 3: [(1, 1)], 5: [(1, 2)], 7: [(1, 3)], 9: [(1, 4)]}
WINS_N = {5: [(1, 0)], 7: [(1, 1)], 9: [(1, 2)], 10: [(1, 3)], 11: [(1, 4)]}


def _sequence():
    tables, wins = [], []
    for slot in range(-1, UNITS + 2):
        for c, g in TABLES_0.get(slot, []):
            tables += [(c, f, slot) for f in (HOT_LATER if c else HOT_FIRST)[g]]
        wins += WINS_0.get(slot, [])
    return tables, wins


SEQ_TABLES, SEQ_WINS = _sequence()


def program(nc, t):
    fp32, bf16, fp16, i32 = mybir.dt.float32, mybir.dt.bfloat16, mybir.dt.float16, mybir.dt.int32
    ALU, ACT = mybir.AluOpType, mybir.ActivationFunctionType
    AX = mybir.AxisListType

    ctx = ExitStack()
    with ctx:
        def sb(name, shape, dt):
            return ctx.enter_context(nc.sbuf_tensor(name, shape, dt))

        def sem(name):
            return ctx.enter_context(nc.semaphore(name))

        banks = [ctx.enter_context(nc.psum_tensor(f"bank{n}", [P, 512], fp32)) for n in range(8)]
        z_bank, o_bank, v_bank, w_bank = banks[0:2], banks[2:4], banks[4], banks[5:8]

        ident = sb("ident", [P, P], fp32)
        h_mask = sb("h_mask", [P, 2 * P], fp32)
        k_mask = sb("k_mask", [P, K], fp32)
        row_no = sb("row_no", [P, KT_ALL], fp32)
        alpha = sb("alpha", [P, FT, K], fp32)
        alpha_r = sb("alpha_r", [P, 2, FT, K], fp32)
        alpha_p = sb("alpha_p", [P, 3, FT, K], bf16)
        w_dk = sb("w_dk", [P, 2, D], fp32)
        hv_dk = sb("hv_dk", [P, 2], fp32)
        v_dk = sb("v_dk", [P, 2, D], fp32)
        v_diag = sb("v_diag", [P, 2, 2 * P], fp32)
        m_w = sb("m_w", [P, FT, 2 * P], fp32)
        table = sb("table", [TP, KT_ALL, D], fp32)
        parts = sb("parts", [TP, KT_ALL, 3, D], bf16)
        ids_all = sb("ids_all", [P, B // P, S], i32)
        ids_now = sb("ids_now", [P, BT, S], i32)
        ids_flat = sb("ids_flat", [P, S * B // P], i32)
        ids_half = sb("ids_half", [P, S * B // P], fp16)
        ids_b = sb("ids_b", [TP, N_LATER, B], fp16)
        ids_b0 = sb("ids_b0", [TP, N_HOT - N_LATER, CH], fp16)
        onehot = sb("onehot", [TP, 2, max(KT.values()), CH], bf16)
        e = sb("e", [P, BT, EC], fp32)
        e_cols = sb("e_cols", [P, BT, FT * P], fp32)
        e_win = sb("e_win", [P, FT, CH], fp32)
        x0 = sb("x0", [P, X_SLOTS, QH * CH], fp32)
        prod = sb("prod", [P, 2, QH * CH], fp32)
        tower = sb("tower", [P, 8 * CH], fp32)
        h1 = tower[:, 0:4 * CH].rearrange("p (a c) -> p a c", a=H1 // P)
        h2 = tower[:, 4 * CH:6 * CH].rearrange("p (a c) -> p a c", a=H2 // P)
        z_t = tower[:, 6 * CH:8 * CH].rearrange("p (a c) -> p a c", a=2)
        n_win = FT * D * 64
        windows_c = tower[:, 0:n_win // 2].bitcast(bf16).rearrange("p (g d c) -> p g d c", g=FT, d=D)
        ab = tower[0:P // 2, n_win // 2:n_win // 2 + FT * 2 * P].rearrange("p (g c) -> p g c", g=FT)
        spare = x0[:, 3:5, :].rearrange("p a c -> p (a c)")
        rest = [spare[0:TP, n * KT_ALL * D:(n + 1) * KT_ALL * D].rearrange("p (k d) -> p k d", d=D) for n in range(2)]
        ab_t = spare[:, 2 * KT_ALL * D:2 * KT_ALL * D + FT * 2 * P].rearrange("p (g a c) -> p g a c", g=FT, a=2)
        ctx_t = sb("ctx_t", [D, B], fp32)
        w1_z = sb("w1_z", [P, 2, H1], fp32)
        w1_c = sb("w1_c", [D, H1], fp32)
        w2 = sb("w2", [P, H1 // P, H2], fp32)
        w3 = sb("w3", [P, H2 // P], fp32)
        b1 = sb("b1", [P, H1 // P], fp32)
        b2 = sb("b2", [P, H2 // P], fp32)
        y_row = sb("y_row", [1, CH], fp32)

        in_ids = sem("in_ids")
        in_ids_flat = sem("in_ids_flat")
        ids_stored = sem("ids_stored")
        in_ids_b = [sem(f"in_ids_b{n}") for n in range(N_HOT)]
        in_row_no = sem("in_row_no")
        in_small = sem("in_small")
        in_alpha = sem("in_alpha")
        in_win = sem("in_win")
        in_tables = sem("in_tables")
        in_tower = sem("in_tower")
        in_x0 = [sem(f"in_x0_{slot}") for slot in range(X_SLOTS)]
        gathered = [sem(f"gathered_{g}") for g in range(FT)]
        y_stored = sem("y_stored")
        ids_cast = sem("ids_cast")
        padded = sem("padded")
        v_made = sem("v_made")
        v_spread = sem("v_spread")
        alpha_split = sem("alpha_split")
        alpha_rest = sem("alpha_rest")
        ab_summed = sem("ab_summed")
        ab_kept = sem("ab_kept")
        ab_turned = sem("ab_turned")
        ab_t_kept = sem("ab_t_kept")
        m_summed = sem("m_summed")
        m_kept = sem("m_kept")
        split = sem("split")
        rest_made = sem("rest_made")
        ids_copied = sem("ids_copied")
        gathers_begun = sem("gathers_begun")
        hot_made = sem("hot_made")
        hot_used = sem("hot_used")
        rows_kept = sem("rows_kept")
        e_spread = sem("e_spread")
        win_turned = sem("win_turned")
        win_kept = sem("win_kept")
        prod_made = sem("prod_made")
        z_summed = sem("z_summed")
        z_kept = sem("z_kept")
        h1_summed = sem("h1_summed")
        h1_made = sem("h1_made")
        h2_summed = sem("h2_summed")
        h2_made = sem("h2_made")
        y_summed = sem("y_summed")
        y_kept = sem("y_kept")

        N_SMALL_LOADS, N_TOWER_LOADS = 5, 7

        def place_table(i, first, c, f):
            if first:
                return [s[:2] for s in SEQ_TABLES].index((c, f))
            return i * N_LATER + (len(SEQ_TABLES) - N_LATER + sum(HOT_LATER, []).index(f))

        def place_window(i, first, c, ft):
            if first:
                return SEQ_WINS.index((c, ft))
            return i * FT + (len(SEQ_WINS) - FT + ft)

        def hot_tables(i, first, slot):
            return [(c, f) for c, g in (TABLES_0 if first else TABLES_N).get(slot, [])
                    for f in (HOT_FIRST if c == 0 else HOT_LATER)[g]]

        def windows_of(first, slot):
            return (WINS_0 if first else WINS_N).get(slot, [])

        def spreads_that_read(i, first, ft):
            return place_window(i, first, 0, min(ft + 1, FT - 1)) + 1 if first else \
                (i - 1) * FT + (len(SEQ_WINS) - FT + min(ft + 1, FT - 1)) + 1

        def place_slot(first, c, f):
            return place_table(0, True, c, f) % 2 if first else sum(HOT_LATER, []).index(f) % 2

        def hot_free(i, first, c, f):
            if first:
                return place_table(0, True, c, f) - 1
            n = sum(HOT_LATER, []).index(f)
            return i * N_LATER + (len(SEQ_TABLES) - N_LATER + max(n - 1, 0))

        def group_of(f):
            return next(g for g in range(FT) if f in NEW[g])

        block = ctx.enter_context(nc.Block())

        @block.sync
        def _(sp):
            def load_x0(unit, slot):
                sp.dma_start(x0[:, slot, :], t["x0"][bass.ds(unit * 2 * CW, 2 * CW), :].unsqueeze(1).to_broadcast(
                    [2 * CW, CW, QH * CH])).then_inc(in_x0[slot], 16)

            sp.dma_start(ids_flat[:], t["ids_t"].rearrange("f (a b) -> (f a) b", b=S * B // P)).then_inc(in_ids_flat, 16)
            sp.dma_start(ids_all[:], t["ids"].rearrange("(t p) f -> p t f", p=P)).then_inc(in_ids, 16)
            sp.dma_start(alpha[:], t["alpha"].rearrange("(g p) k -> p g k", p=P)).then_inc(in_alpha, 16)
            sp.dma_start(windows_c, t["windows_c"].bitcast(bf16)).then_inc(in_win, 16)
            sp.wait_ge(ids_stored, 16)
            for f in sum(HOT_FIRST, []):
                n = HOT.index(f)
                row = t["ids_half"][f:f + 1, :]
                if n < N_LATER:
                    sp.dma_start(ids_b[:, n, :], row.to_broadcast([TP, B])).then_inc(in_ids_b[n], 16)
                else:
                    sp.dma_start(ids_b0[:, n - N_LATER, :], row[:, 0:CH].to_broadcast([TP, CH])).then_inc(in_ids_b[n], 16)
            for unit in range(3):
                load_x0(unit, unit)
            sp.dma_start(w1_z[:], t["w1_z"].rearrange("(a p) n -> p a n", p=P)).then_inc(in_tower, 16)
            sp.dma_start(w1_c[:], t["w1_c"]).then_inc(in_tower, 16)
            sp.dma_start(ctx_t[:], t["ctx_t"]).then_inc(in_tower, 16)
            sp.dma_start(b1[:], t["b1"]).then_inc(in_tower, 16)
            sp.wait_ge(split, 3)
            sp.wait_ge(m_summed, (FT + 1) // 2)
            for unit in range(3, X_SLOTS):
                load_x0(unit, unit)
            sp.dma_start(w2[:], t["w2"].rearrange("(a p) n -> p a n", p=P)).then_inc(in_tower, 16)
            sp.dma_start(b2[:], t["b2"]).then_inc(in_tower, 16)
            sp.dma_start(w3[:], t["w3"]).then_inc(in_tower, 16)

            def reload_x0(i, u):
                sp.wait_ge(prod_made, i * UNITS + u + 1)
                load_x0(i * UNITS + u + X_SLOTS, u % X_SLOTS)

            with sp.Fori(0, NCH - 1) as i:
                for u in range(UNITS):
                    reload_x0(i, u)
            for u in range(UNITS - X_SLOTS):
                reload_x0(NCH - 1, u)

        @block.gpsimd
        def _(pool):
            def gathers(g, hot):
                for f in NEW[g]:
                    if f not in hot:
                        for bt in range(BT):
                            nc.gpsimd.indirect_dma_start(
                                out=e[:, bt, f * D:(f + 1) * D], out_offset=None, in_=t[f"tbl_{f}"][:, :],
                                in_offset=bass.IndirectOffsetOnAxis(ap=ids_now[:, bt, f:f + 1], axis=0)
                            ).then_inc(gathered[g], 16)

            def per_chunk(g):
                return 16 * BT * (len(NEW[g]) - len(HOT_LATER[g]))

            def in_first(g):
                return 16 * BT * (len(NEW[g]) - len(HOT_FIRST[g]))

            pool.wait_ge(in_ids, 16)
            nc.gpsimd.tensor_copy(ids_now[:], ids_all[:, 0:BT, :]).then_inc(ids_copied, 1)
            pool.wait_ge(ids_copied, 1)
            for g in range(FT):
                gathers(g, HOT_FIRST[g])

            def chunk_gathers(c, second):
                for g in range(FT):
                    fields = slice(NEW[g][0], NEW[g][-1] + 1)
                    pool.wait_ge(gathered[g], (c - 1) * per_chunk(g) + in_first(g))
                    pool.sem_inc(gathers_begun, 1)
                    nc.gpsimd.tensor_copy(ids_now[:, :, fields], ids_all[:, bass.ds(c * BT, BT), fields]).then_inc(ids_copied, 1)
                    pool.wait_ge(e_spread, spreads_that_read(c - 1, second, g))
                    pool.sem_inc(gathers_begun, 1)
                    pool.wait_ge(ids_copied, (c - 1) * FT + g + 2)
                    pool.sem_inc(gathers_begun, 1)
                    gathers(g, HOT_LATER[g])

            chunk_gathers(1, True)
            with pool.Fori(2, NCH) as c:
                chunk_gathers(c, False)

        @block.vector
        def _(dve):
            def make_hot(i, first, c, f):
                at = place_table(i, first, c, f)
                slot = place_slot(first, c, f)
                if not first or at >= 2:
                    dve.wait_ge(hot_used, hot_free(i, first, c, f))
                n = HOT.index(f)
                if first and c == 0:
                    dve.wait_ge(in_ids_b[n], 16)
                    ids = ids_b[:, n, 0:CH] if n < N_LATER else ids_b0[:, n - N_LATER, :]
                else:
                    ids = ids_b[:, n, bass.ds((i + 1) * CH, CH)]
                for k in range(KT[f]):
                    last = nc.vector.tensor_scalar(onehot[:, slot, k, :], ids, row_no[0:TP, KT_AT[f] + k:KT_AT[f] + k + 1],
                                                   None, ALU.is_equal)
                last.then_inc(hot_made, 1)

            def keep_rows(i, first, c, f):
                dve.wait_ge(hot_used, place_table(i, first, c, f) + 1)
                if not (first and c == 0):
                    dve.wait_ge(e_spread, spreads_that_read(i, first, group_of(f)))
                parts_ps = o_bank[place_slot(first, c, f)][:, 0:BT * 3 * D].rearrange("p (b s d) -> p b d s", b=BT, s=3)
                nc.vector.tensor_reduce(e[:, :, f * D:(f + 1) * D], parts_ps, AX.X, ALU.add).then_inc(rows_kept, 1)

            dve.wait_ge(in_ids_flat, 16)
            nc.vector.tensor_scalar(ids_half[:], ids_flat[:], 2048.0, None, ALU.min).then_inc(ids_cast, 1)
            nc.vector.memset(e[:, :, S * D:], 0.0).then_inc(padded, 1)
            for n in range(2):
                dve.wait_ge(alpha_split, n + 1)
                nc.vector.tensor_tensor(alpha_r[:, n, :, :], alpha[:] if n == 0 else alpha_r[:, 0, :, :],
                                        alpha_p[:, n, :, :], ALU.subtract).then_inc(alpha_rest, 1)
                if n == 0:
                    dve.wait_ge(alpha_rest, 1)
            for n in range(2):
                dve.wait_ge(split, n + 1)
                if n == 1:
                    dve.wait_ge(rest_made, 1)
                nc.vector.tensor_tensor(rest[n], table[:] if n == 0 else rest[0], parts[:, :, n, :],
                                        ALU.subtract).then_inc(rest_made, 1)
            dve.wait_ge(in_row_no, 16)
            pending = []

            def keep_pending(i, first, keep_if):
                for item in [x for x in pending if keep_if(x)]:
                    pending.remove(item)
                    keep_rows(i, first, item[1], item[2])

            def make_tables(i, first, slot):
                for c, f in hot_tables(i, first, slot):
                    if first:
                        place = place_table(0, True, c, f)
                        keep_pending(i, first, lambda x: x[0] <= place - 2)
                    else:
                        place = sum(HOT_LATER, []).index(f)
                    make_hot(i, first, c, f)
                    pending.append((place, c, f, slot))

            dve.wait_ge(in_small, 16 * N_SMALL_LOADS)
            for a in range(2):
                last = nc.vector.tensor_scalar(v_dk[:, a, :], w_dk[:, a, :], hv_dk[:, a:a + 1], None, ALU.mult)
            last.then_inc(v_made, 1)
            dve.wait_ge(v_made, 1)
            for a in range(2):
                last = nc.vector.tensor_tensor(
                    v_diag[:, a, :].rearrange("p (g k h) -> p g k h", g=HP, k=K),
                    v_dk[:, a, :].rearrange("p (g h) -> p g h", g=HP).unsqueeze(2).to_broadcast([P, HP, K, 2]),
                    k_mask[:].unsqueeze(1).unsqueeze(3).to_broadcast([P, HP, K, 2]), ALU.mult)
            last.then_inc(v_spread, 1)
            make_tables(0, True, -1)
            for ft in range(0, FT, 2):
                n = min(2, FT - ft)
                dve.wait_ge(m_summed, ft // 2 + 1)
                src = w_bank[ft // 2][:, 0:n * 2 * P].rearrange("p (a c) -> p a c", a=n)
                nc.vector.tensor_tensor(m_w[:, ft:ft + n, :], src, h_mask[:].unsqueeze(1).to_broadcast([P, n, 2 * P]),
                                        ALU.mult).then_inc(m_kept, 1)
            keep_pending(0, True, lambda x: True)

            def chunk_units(i, first, more):
                for u in range(UNITS):
                    ft = u // 2
                    dve.wait_ge(in_x0[u % X_SLOTS], i * 32 + 16 * (u // X_SLOTS + 1))
                    if u % 2 == 0:
                        dve.wait_ge(win_kept, place_window(i, True, 0, ft) + 1 if first
                                    else (i - 1) * FT + (len(SEQ_WINS) - FT + ft) + 1)
                    if not first or u >= 2:
                        dve.wait_ge(z_summed, i * UNITS + u - 1)
                    nc.vector.tensor_tensor(
                        prod[:, u % 2, :].rearrange("p (q b) -> p q b", q=QH),
                        x0[:, u % X_SLOTS, :].rearrange("p (q b) -> p q b", q=QH),
                        e_win[:, ft, :].unsqueeze(1).to_broadcast([P, QH, CH]), ALU.mult).then_inc(prod_made, 1)
                    if more:
                        make_tables(i, first, u)
                        keep_pending(i, first, lambda x: x[3] < u)
                if more:
                    keep_pending(i, first, lambda x: True)

            chunk_units(0, True, True)
            with dve.Fori(1, NCH - 1) as i:
                chunk_units(i, False, True)
            chunk_units(NCH - 1, False, False)

        @block.scalar
        def _(act):
            act.dma_start(row_no[:], t["row_no"]).then_inc(in_row_no, 16)
            for f in HOT:
                act.dma_start(table[:, KT_AT[f]:KT_AT[f] + KT[f], :],
                              t[f"tbl_{f}"].rearrange("(p k) d -> p k d", p=TP)).then_inc(in_tables, 16)
            act.wait_ge(ids_cast, 1)
            act.dma_start(t["ids_half"].rearrange("f (a b) -> (f a) b", b=S * B // P), ids_half[:]).then_inc(ids_stored, 16)
            act.dma_start(ident[:], t["ident"]).then_inc(in_small, 16)
            act.dma_start(k_mask[:], t["k_mask"]).then_inc(in_small, 16)
            act.dma_start(h_mask[:], t["h_mask"]).then_inc(in_small, 16)
            act.dma_start(w_dk[:], t["w_dk"].rearrange("(a p) h -> p a h", p=P)).then_inc(in_small, 16)
            act.dma_start(hv_dk[:], t["hv_dk"]).then_inc(in_small, 16)
            act.wait_ge(in_alpha, 16)
            nc.scalar.copy(alpha_p[:, 0, :, :], alpha[:]).then_inc(alpha_split, 1)
            for n in range(2):
                act.wait_ge(alpha_rest, n + 1)
                nc.scalar.copy(alpha_p[:, n + 1, :, :], alpha_r[:, n, :, :]).then_inc(alpha_split, 1)
            act.wait_ge(in_tables, 16 * N_HOT)
            nc.scalar.copy(parts[:, :, 0, :], table[:]).then_inc(split, 1)
            for n in range(2):
                act.wait_ge(rest_made, n + 1)
                nc.scalar.copy(parts[:, :, n + 1, :], rest[n]).then_inc(split, 1)
            for ft in range(0, FT, 2):
                n = min(2, FT - ft)
                act.wait_ge(ab_summed, ft // 2 + 1)
                nc.scalar.copy(ab[:, ft:ft + n, :].rearrange("p a c -> p (a c)"),
                               w_bank[ft // 2][0:P // 2, 0:n * 2 * P]).then_inc(ab_kept, 1)
            for ft in range(0, FT, 2):
                n = min(2, FT - ft)
                act.wait_ge(ab_turned, ft // 2 + 1)
                src = (o_bank + [v_bank])[ft // 2][:, 0:n * P].rearrange("p (m c) -> p m c", c=CW)
                nc.scalar.copy(ab_t[:, ft:ft + n, :, :].rearrange("p a s (f h c) -> p (a s f) h c", h=2, c=CW),
                               src.unsqueeze(2).to_broadcast([P, n * 2 * 8, 2, CW])).then_inc(ab_t_kept, 1)

            def spread_e(i, first, c, ft):
                hot = (HOT_FIRST if first and c == 0 else HOT_LATER)[ft]
                act.wait_ge(rows_kept, place_table(i, first, c, hot[-1]) + 1)
                begun = BT * (len(NEW[ft]) - len(HOT_FIRST[ft]))
                if not (first and c == 0):
                    begun = (i + 1) * (BT * (len(NEW[ft]) - len(HOT_LATER[ft]))) + begun
                act.wait_ge(gathered[ft], begun * 16)
                if first and c == 0:
                    act.wait_ge(padded, 1)
                else:
                    act.wait_ge(win_turned, place_window(0, True, 0, ft) + 1 if first
                                else (i - 1) * FT + (len(SEQ_WINS) - FT + ft) + 1)
                base, inner = WINDOWS[ft]
                for lo in range(2):
                    for bt in range(BT):
                        src = bass.AP(e, bt * EC + base + inner * lo, [[BT * EC, P], [13, 4], [0, 2], [1, CW]])
                        dst = bass.AP(e_cols, bt * FT * P + ft * P + 2 * CW * lo,
                                      [[BT * FT * P, P], [4 * CW, 4], [CW, 2], [1, CW]])
                        last = nc.scalar.copy(dst, src)
                last.then_inc(e_spread, 1)

            def keep_windows(i, first, c, ft):
                act.wait_ge(win_turned, place_window(i, first, c, ft) + 1)
                if not (first and c == 0):
                    act.wait_ge(prod_made, i * UNITS + 2 * ft + 2)
                nc.scalar.copy(e_win[:, ft, :], v_bank[:]).then_inc(win_kept, 1)

            spread_e(0, True, 0, 0)
            keep_windows(0, True, 0, 0)
            act.wait_ge(in_tower, 16 * N_TOWER_LOADS)

            def chunk_rest(i, first, more):
                def windows(slot, spread_only=False, keep_only=False):
                    for c, ft in (windows_of(first, slot) if more or slot < 0 else []):
                        if not keep_only:
                            spread_e(i, first, c, ft)
                        if not spread_only:
                            keep_windows(i, first, c, ft)

                def keep_z(half):
                    act.wait_ge(z_summed, i * UNITS + UNITS - 1 + half)
                    nc.scalar.copy(z_t[:, half, :], z_bank[half][:]).then_inc(z_kept, 1)

                for u in range(UNITS - 1):
                    windows(u)
                windows(UNITS - 1, spread_only=True)
                keep_z(0)
                keep_z(1)
                windows(UNITS - 1, keep_only=True)
                windows(UNITS)
                for m in range(H1 // P):
                    act.wait_ge(h1_summed, i * (H1 // P) + m + 1)
                    nc.scalar.activation(h1[:, m, :], w_bank[m % 3][:], ACT.Relu, bias=b1[:, m:m + 1]).then_inc(h1_made, 1)
                windows(UNITS + 1, spread_only=True)
                for n in range(H2 // P):
                    act.wait_ge(h2_summed, i * (H2 // P) + n + 1)
                    nc.scalar.activation(h2[:, n, :], w_bank[n + 1][:], ACT.Relu, bias=b2[:, n:n + 1]).then_inc(h2_made, 1)
                windows(UNITS + 1, keep_only=True)
                act.wait_ge(y_summed, i + 1)
                if not first:
                    act.wait_ge(y_stored, i * 16)
                nc.scalar.copy(y_row[:], w_bank[0][0:1, :]).then_inc(y_kept, 1)
                act.wait_ge(y_kept, i + 1)
                act.dma_start(t["out"][bass.ds(i, 1), :], y_row[:]).then_inc(y_stored, 16)

            chunk_rest(0, True, True)
            with act.Fori(1, NCH - 1) as i:
                chunk_rest(i, False, True)
            chunk_rest(NCH - 1, False, False)
            act.wait_ge(y_stored, 16 * NCH)

        @block.tensor
        def _(pe):
            def table_rows(i, first, slot):
                for c, f in hot_tables(i, first, slot):
                    at = place_table(i, first, c, f)
                    pe.wait_ge(hot_made, at + 1)
                    if not first or at >= 2:
                        pe.wait_ge(rows_kept, hot_free(i, first, c, f))
                    half = place_slot(first, c, f)
                    for bt in range(BT):
                        for k in range(KT[f]):
                            last = nc.tensor.matmul(o_bank[half][:, bt * 3 * D:(bt + 1) * 3 * D],
                                                    onehot[:, half, k, bt * P:(bt + 1) * P],
                                                    parts[:, KT_AT[f] + k, :, :].rearrange("p s d -> p (s d)"),
                                                    start=k == 0, stop=k == KT[f] - 1)
                    last.then_inc(hot_used, 1)

            def turn_windows(i, first, slot):
                for c, ft in windows_of(first, slot):
                    at = place_window(i, first, c, ft)
                    pe.wait_ge(e_spread, at + 1)
                    if not first or at >= 1:
                        pe.wait_ge(win_kept, at)
                    for bt in range(BT):
                        last = nc.tensor.transpose(v_bank[:, bt * P:(bt + 1) * P], e_cols[:, bt, ft * P:(ft + 1) * P], ident[:])
                    last.then_inc(win_turned, 1)

            pe.wait_ge(alpha_split, 3)
            pe.wait_ge(in_win, 16)
            for ft in range(FT):
                for d in range(D):
                    at = (ft % 2) * 2 * P + d * K
                    for n in range(3):
                        last = nc.tensor.matmul(w_bank[ft // 2][0:P // 2, at:at + K], windows_c[:, ft, d, :],
                                                alpha_p[:, n, ft, :], start=n == 0, stop=n == 2)
                if ft % 2 or ft == FT - 1:
                    last.then_inc(ab_summed, 1)
            pe.wait_ge(in_small, 16 * N_SMALL_LOADS)
            for ft in range(FT):
                if ft % 2 == 0:
                    pe.wait_ge(ab_kept, ft // 2 + 1)
                for a in range(2):
                    at = (ft % 2 * 2 + a) * (P // 2)
                    last = nc.tensor.transpose((o_bank + [v_bank])[ft // 2][:, at:at + P // 2],
                                               ab[:, ft, a * P:(a + 1) * P], ident[0:P // 2, 0:P // 2])
                if ft % 2 or ft == FT - 1:
                    last.then_inc(ab_turned, 1)
            pe.wait_ge(v_spread, 1)
            for ft in range(FT):
                if ft % 2 == 0:
                    pe.wait_ge(ab_t_kept, ft // 2 + 1)
                at = ft % 2 * 2 * P
                for a in range(2):
                    last = nc.tensor.matmul(w_bank[ft // 2][:, at:at + 2 * P], ab_t[:, ft, a, :], v_diag[:, a, :],
                                            start=a == 0, stop=a == 1)
                if ft % 2 or ft == FT - 1:
                    last.then_inc(m_summed, 1)
            pe.wait_ge(split, 3)
            table_rows(0, True, -1)
            turn_windows(0, True, -1)
            pe.wait_ge(m_kept, (FT + 1) // 2)

            def contract(i, u):
                ft, half = divmod(u, 2)
                pe.wait_ge(prod_made, i * UNITS + u + 1)
                for q in range(QH):
                    at = (QH * half + q) * ZW
                    last = nc.tensor.matmul(z_bank[half][q * ZW:(q + 1) * ZW, :], m_w[:, ft, at:at + ZW],
                                            prod[:, u % 2, q * CH:(q + 1) * CH], start=ft == 0, stop=ft == FT - 1)
                last.then_inc(z_summed, 1)

            def tower_all(i, first, more):
                def layer1(m, steps):
                    for step in steps:
                        if step == 0 and m == 0 and not first:
                            pe.wait_ge(y_kept, i)
                        if step == 0 and m == 3:
                            pe.wait_ge(h1_made, i * (H1 // P) + 1)
                        if step < 2:
                            w, x = w1_z[:, step, m * P:(m + 1) * P], z_t[:, step, :]
                        else:
                            w, x = w1_c[:, m * P:(m + 1) * P], ctx_t[:, bass.ds(i * CH, CH)]
                        last = nc.tensor.matmul(w_bank[m % 3][:], w, x, start=step == 0, stop=step == 1)
                    return last

                if first:
                    pe.wait_ge(in_tower, 16 * N_TOWER_LOADS)
                pe.wait_ge(z_kept, i * 2 + 1)
                for m in range(2):
                    layer1(m, (0, 2))
                if more:
                    turn_windows(i, first, UNITS)
                pe.wait_ge(z_kept, i * 2 + 2)
                for m in range(2):
                    layer1(m, (1,)).then_inc(h1_summed, 1)
                for m in range(2, H1 // P):
                    layer1(m, (0, 2, 1)).then_inc(h1_summed, 1)
                for n in range(H2 // P):
                    for m in range(H1 // P):
                        if n == 0 and m in (0, 3):
                            pe.wait_ge(h1_made, i * (H1 // P) + max(m, 2) + 1)
                        last = nc.tensor.matmul(w_bank[n + 1][:], w2[:, m, n * P:(n + 1) * P], h1[:, m, :],
                                                start=m == 0, stop=m == H1 // P - 1)
                    last.then_inc(h2_summed, 1)
                if more:
                    turn_windows(i, first, UNITS + 1)
                for n in range(H2 // P):
                    pe.wait_ge(h2_made, i * (H2 // P) + n + 1)
                    last = nc.tensor.matmul(w_bank[0][0:1, :], w3[:, n:n + 1], h2[:, n, :], start=n == 0, stop=n == 1)
                last.then_inc(y_summed, 1)

            def chunk_all(i, first, more):
                for u in range(UNITS):
                    contract(i, u)
                    if more:
                        if first:
                            turn_windows(i, first, u)
                        table_rows(i, first, u)
                        if not first:
                            turn_windows(i, first, u)
                tower_all(i, first, more)

            chunk_all(0, True, True)
            with pe.Fori(1, NCH - 1) as i:
                chunk_all(i, False, True)
            chunk_all(NCH - 1, False, False)


def _constants():
    import numpy as np
    part = np.arange(P)
    windows_c = np.zeros((P, FT, D, 8, CW), np.uint16)
    for f in range(F):
        for g in range(256):
            j, d = divmod(g, D)
            windows_c[(f % 8) * 16 + j, f // 8, d, f % 8, (256 * f + g) // F - window_start(f)] = 0x3F80
    h_mask = ((part[:, None] // CW) % 2 == np.arange(2 * P)[None, :] % 2).astype(np.float32)
    k_mask = (part[:, None] % K == np.arange(K)[None, :]).astype(np.float32)
    row_no = np.concatenate([part[:, None] * KT[f] + np.arange(KT[f])[None, :] for f in HOT], axis=1).astype(np.float32)
    return {"windows_c": windows_c.reshape(P, FT, D, 64), "h_mask": h_mask, "k_mask": k_mask,
            "row_no": row_no, "ident": np.eye(P, dtype=np.float32)}


def kernel(**inputs):
    import numpy as np
    import concourse.bacc as bacc
    from concourse.bass_utils import run_bass_kernel_spmd

    a = {name: np.asarray(value) for name, value in inputs.items()}
    w1 = a["W_top1"]
    x0 = np.concatenate([a["r_x0"], np.zeros((B, 8 * FT - F, D), np.float32)], axis=1)
    x0 = x0.reshape(NCH, CH, FT, 8, 2, QH, 2).transpose(0, 2, 4, 3, 6, 5, 1)
    arrays = _constants()
    arrays.update({f"tbl_{f}": a[f"tbl_{f}"] for f in range(S)})
    arrays.update({
        "ids": a["ids"], "ids_t": a["ids"].T, "x0": x0.reshape(NCH * UNITS * 2 * CW, QH * CH), "ctx_t": a["dense_ctx"].T,
        "alpha": np.concatenate([a["L0_rec_alpha"], np.zeros((P * FT - S * F, K), np.float32)]),
        "w_dk": a["L0_rec_w"].transpose(2, 0, 1).reshape(D * K, D),
        "hv_dk": a["L0_rec_hv"].transpose(1, 0, 2).reshape(2, P).T,
        "w1_z": w1[0:K * D].reshape(K, HP, 2, H1).transpose(1, 0, 2, 3).reshape(K * D, H1), "w1_c": w1[K * D:],
        "b1": a["b_top1"].reshape(H1 // P, P).T, "w2": a["W_top2"], "b2": a["b_top2"].reshape(H2 // P, P).T,
        "w3": a["W_top3"].reshape(H2 // P, P).T,
    })
    arrays = {f"{name}_dram": np.ascontiguousarray(value) for name, value in arrays.items()}

    nc = bacc.Bacc("TRN2", target_bir_lowering=False, num_devices=1)
    t = {name.removesuffix("_dram"): nc.dram_tensor(name, value.shape, mybir.dt.from_np(value.dtype), kind="ExternalInput").ap()
         for name, value in arrays.items()}
    t["ids_half"] = nc.dram_tensor("ids_half_dram", (S, B), mybir.dt.float16).ap()
    out = nc.dram_tensor("out_dram", (B, 1), mybir.dt.float32, kind="ExternalOutput").ap()
    t["out"] = out.rearrange("(c b) o -> c (b o)", c=NCH)
    program(nc, t)
    return run_bass_kernel_spmd(nc, [arrays], core_ids=[0]).results[0]["out_dram"]
```

```python
from contextlib import ExitStack

import concourse.bass as bass
from concourse import mybir

B, F, S, D, K = 2048, 39, 16, 16, 16
P = 128
BT = 4
CH = BT * P
NCH = B // CH
FT = (F + 7) // 8
HP = D // 2
QH = HP // 2
HB = CH // 2
UNITS = 2 * FT
X_SLOTS = 5
CW = 8
ZW = 2 * K
VOCAB = [12500, 1250, 1250, 125000, 1000, 1250, 12500, 1000, 12500, 125000, 1000, 12500, 1250, 1000, 125000, 1000]
TP = 125
NEW = [[0, 1, 2, 3], [4, 5, 6], [7, 8, 9], [10, 11, 12, 13], [14, 15]]
PAIRS = [(1, 2), (4, 5), (7, 10), (13, 15)]
NP = len(PAIRS)
HOT = [7, 10, 13, 15, 4, 5, 1, 2]
HEAD_TABLES = list(PAIRS[0])
TABLES = HEAD_TABLES + [f for f in HOT if f not in HEAD_TABLES]
KT = {f: VOCAB[f] // TP for f in HOT}
KT_AT = {f: sum(KT[g] for g in TABLES[:n]) for n, f in enumerate(TABLES)}
KT_ALL = sum(KT.values())
HEAD = sum(KT[f] for f in HEAD_TABLES)
SIZES = [(0, 5, 8), (5, 8, 10)]
assert all(KT[f] == size for lo, hi, size in SIZES for f in HOT[lo:hi])
H1, H2 = 512, 256


def _windows():
    found = []
    for ft in range(FT):
        fs = range(8 * ft, min(8 * ft + 8, F))
        found.append(next((base, inner) for base in range(S * D) for inner in range(4, 9)
                          if all(0 <= 256 * f // F - (base + 13 * (f % 8 // 2) + inner * (f % 2))
                                 and (256 * f + 255) // F - (base + 13 * (f % 8 // 2) + inner * (f % 2)) < CW
                                 for f in fs)))
    return found


WINDOWS = _windows()


def window_start(f):
    base, inner = WINDOWS[f // 8]
    return base + 13 * (f % 8 // 2) + inner * (f % 2)


AT_IDENT, AT_H_MASK, AT_K_MASK, AT_ROW = 0, P, 3 * P, 3 * P + K
N_CONSTS = AT_ROW + len(SIZES)
EC = max(window_start(f) for f in range(8 * FT)) + CW

PAIRS_0 = {-1: [(0, 0), (0, 1)], 0: [(0, 2)], 1: [(0, 3)], 2: [(1, 0)], 3: [(1, 1)], 5: [(1, 2)], 6: [(1, 3)]}
SPREADS_0 = {-1: [(0, 0)], 0: [(0, 1)], 1: [(0, 2)], 2: [(0, 3)], 3: [(0, 4)], 4: [(1, 0)], 5: [(1, 1)], 6: [(1, 2)],
             7: [(1, 3)], 8: [(1, 4)]}
WINS_0 = {-1: [(0, 0)], 0: [(0, 1)], 1: [(0, 2)], 2: [(0, 3)], 3: [(0, 4)], 5: [(1, 0)], 6: [(1, 1)], 7: [(1, 2)],
          8: [(1, 3)], 9: [(1, 4)]}
PAIRS_N = {0: [(1, 0)], 1: [(1, 1)], 3: [(1, 2)], 4: [(1, 3)]}
SPREADS_N = {3: [(1, 0)], 4: [(1, 1)], 5: [(1, 2)], 6: [(1, 3)], 8: [(1, 4)]}
WINS_N = {5: [(1, 0)], 6: [(1, 1)], 7: [(1, 2)], 8: [(1, 3)], 9: [(1, 4)]}
_MATMULS = [("layer1", m, k) for m in range(H1 // P) for k in (2, 3, 0, 1)] + \
           [("layer2", m, k) for m in range(H2 // P) for k in range(H1 // P)] + [("layer3", 0, k) for k in range(H2 // P)]
TOWER_STEPS = [_MATMULS[0:7], _MATMULS[7:14], _MATMULS[14:18], _MATMULS[18:22], _MATMULS[24:]]
BEFORE_FIFTH = _MATMULS[22:24]
FIRST_INPUT = {"layer1": 2, "layer2": 0, "layer3": 0}
CB = 8
CW1, CX = H1 // CB, B // CB
STACK_X = [0, 0, 0, 1, 1, 1, 2, 2]
LAST_INPUT = {"layer1": 1, "layer2": H1 // P - 1, "layer3": H2 // P - 1}
L1_BANK, L2_BANK, Y_BANK = [1, 2, 0, 1], [2, 0], 2


def program(nc, t):
    fp32, bf16, fp16, i32 = mybir.dt.float32, mybir.dt.bfloat16, mybir.dt.float16, mybir.dt.int32
    ALU, ACT = mybir.AluOpType, mybir.ActivationFunctionType
    AX = mybir.AxisListType

    ctx = ExitStack()
    with ctx:
        def sb(name, shape, dt):
            return ctx.enter_context(nc.sbuf_tensor(name, shape, dt))

        def sem(name):
            return ctx.enter_context(nc.semaphore(name))

        banks = [ctx.enter_context(nc.psum_tensor(f"bank{n}", [P, 512], fp32)) for n in range(8)]
        z_bank, o_bank, v_bank, w_bank = banks[0:2], banks[2:4], banks[4], banks[5:8]

        consts = sb("consts", [P, N_CONSTS], fp32)
        ident = consts[:, AT_IDENT:AT_IDENT + P]
        h_mask = consts[:, AT_H_MASK:AT_H_MASK + 2 * P]
        k_mask = consts[:, AT_K_MASK:AT_K_MASK + K]
        alpha = sb("alpha", [P, FT, K], fp32)
        alpha_r = sb("alpha_r", [P, 2, FT, K], fp32)
        alpha_p = sb("alpha_p", [P, FT, 3, K], bf16)
        w_hv = sb("w_hv", [P, 2, D + 1], fp32)
        v_dk = sb("v_dk", [P, 2, D], fp32)
        v_diag = sb("v_diag", [P, 2, 2 * P], fp32)
        m_w = sb("m_w", [P, FT, 2 * P], fp32)
        table = sb("table", [TP, KT_ALL, D], fp32)
        parts = sb("parts", [TP, KT_ALL, 3, D], bf16)
        ids_all = sb("ids_all", [P, B // P, S], i32)
        ids_now = sb("ids_now", [P, BT, S], i32)
        ids_flat = sb("ids_flat", [P, S * B // P], i32)
        ids_half = sb("ids_half", [P, S * B // P], fp16)
        ids_b = sb("ids_b", [TP, len(HOT), (NCH - 1) * CH], fp16)
        ids_b0 = ids_b[:, :, (NCH - 2) * CH:]
        onehot = sb("onehot", [TP, 2, 2, max(KT.values()), CH], bf16)
        e = sb("e", [P, BT, EC], fp32)
        e_cols = sb("e_cols", [P, BT, FT * P], fp32)
        e_win = sb("e_win", [P, FT, CH], fp32)
        x0 = sb("x0", [P, X_SLOTS, HP * HB], fp32)
        tower = sb("tower", [P, FT * D // 4 * P + FT * P], fp32)
        h1 = tower[:, 0:4 * HB].rearrange("p (a c) -> p a c", a=H1 // P)
        h2 = tower[:, 4 * HB:6 * HB].rearrange("p (a c) -> p a c", a=H2 // P)
        z_t = tower[:, 6 * HB:8 * HB].rearrange("p (a c) -> p a c", a=2)
        n_win = FT * D // 2 * P
        windows_c = tower[:, 0:n_win // 2].bitcast(bf16).rearrange("p (g d c) -> p g d c", g=FT, d=D // 2)
        ab = tower[:, n_win // 2:n_win // 2 + FT * P].rearrange("p (g c) -> p g c", g=FT)
        rest_1 = sb("rest_1", [TP, 2, HEAD, D], fp32)
        spare = x0[:, 3:5, :].rearrange("p a c -> p (a c)")
        n_rest = (KT_ALL - HEAD) * D
        rest = [spare[0:TP, n * n_rest:(n + 1) * n_rest].rearrange("p (k d) -> p k d", d=D) for n in range(2)]
        ab_t = spare[:, 2 * n_rest:2 * n_rest + FT * 2 * P].rearrange("p (g a c) -> p g a c", g=FT, a=2)
        w1_ctx = sb("w1_ctx", [P, CW1 + CX], fp32)
        w1_ctx_rest = sb("w1_ctx_rest", [P, 2, CW1 + CX], fp32)
        w1_ctx_p = sb("w1_ctx_p", [P, 3, CW1 + CX], bf16)
        ctx_stack = sb("ctx_stack", [P, B], bf16)
        w1_stack = sb("w1_stack", [P, H1], bf16)
        ctx_low = sb("ctx_low", [D, B], bf16)
        w1_low = sb("w1_low", [D, H1], bf16)
        w1_z = sb("w1_z", [P, 2, H1], fp32)
        w2 = sb("w2", [P, H1 // P, H2], fp32)
        b_w3 = sb("b_w3", [P, (H1 + 2 * H2) // P], fp32)
        b1, b2, w3 = b_w3[:, 0:H1 // P], b_w3[:, H1 // P:(H1 + H2) // P], b_w3[:, (H1 + H2) // P:]
        y_row = sb("y_row", [1, HB], fp32)

        in_ids = sem("in_ids")
        in_ids_flat = sem("in_ids_flat")
        ids_stored = sem("ids_stored")
        in_ids_b0 = [sem(f"in_ids_b0_{n}") for n in range(2)]
        in_ids_b = [sem(f"in_ids_b_{n}") for n in range(1, NCH)]
        ids_rel = sem("ids_rel")
        in_small = sem("in_small")
        in_alpha = sem("in_alpha")
        in_win = sem("in_win")
        in_table_1 = sem("in_table_1")
        in_tables = sem("in_tables")
        in_tower = sem("in_tower")
        in_x0 = [sem(f"in_x0_{slot}") for slot in range(X_SLOTS)]
        gathered = [sem(f"gathered_{g}") for g in range(FT)]
        y_stored = sem("y_stored")
        in_ctx = sem("in_ctx")
        ctx_split = sem("ctx_split")
        ctx_rest = sem("ctx_rest")
        ctx_stored = sem("ctx_stored")
        ids_cast = sem("ids_cast")
        padded = sem("padded")
        v_made = sem("v_made")
        v_spread = sem("v_spread")
        alpha_split = sem("alpha_split")
        alpha_rest = sem("alpha_rest")
        ab_summed = sem("ab_summed")
        ab_kept = sem("ab_kept")
        ab_turned = sem("ab_turned")
        ab_t_kept = sem("ab_t_kept")
        m_summed = sem("m_summed")
        m_kept = sem("m_kept")
        split_1 = sem("split_1")
        rest_1_made = sem("rest_1_made")
        split = sem("split")
        rest_made = sem("rest_made")
        ids_copied = sem("ids_copied")
        gathers_begun = sem("gathers_begun")
        hot_made = sem("hot_made")
        hot_used = sem("hot_used")
        rows_kept = sem("rows_kept")
        e_spread = sem("e_spread")
        win_turned = sem("win_turned")
        win_kept = sem("win_kept")
        prod_made = sem("prod_made")
        z_summed = sem("z_summed")
        z_kept = sem("z_kept")
        h1_summed = sem("h1_summed")
        h1_made = sem("h1_made")
        h2_summed = sem("h2_summed")
        h2_made = sem("h2_made")
        y_summed = sem("y_summed")
        y_kept = sem("y_kept")

        N_REST = len(HOT) - len(HEAD_TABLES)
        PER_CHUNK = [16 * BT * sum(f not in HOT for f in NEW[g]) for g in range(FT)]
        N_SMALL_LOADS, N_TOWER_LOADS = 2, 3 + 3 + 2 + 2

        def of_slot(plans, first, more, slot):
            return [x for x in plans[0 if first else 1].get(slot, []) if more or x[0] == 0]

        pairs, spreads, windows = (PAIRS_0, PAIRS_N), (SPREADS_0, SPREADS_N), (WINS_0, WINS_N)

        def group_of(f):
            return next(g for g in range(FT) if f in NEW[g])

        def pairs_before(g):
            return max(n + 1 for n, pair in enumerate(PAIRS) if any(group_of(f) <= g for f in pair))

        def spreads_that_read(g):
            return min(g + 1, FT - 1) + 1

        ab_bank = w_bank + o_bank
        turned_bank = [v_bank, z_bank[0], z_bank[1], w_bank[0], w_bank[1]]
        m_bank = [w_bank[2], w_bank[0], w_bank[1]]

        block = ctx.enter_context(nc.Block())

        @block.sync
        def _(sp):
            def load_x0(unit, slot):
                sp.dma_start(x0[:, slot, :], t["x0"][bass.ds(unit * 2 * CW, 2 * CW), :].unsqueeze(1).to_broadcast(
                    [2 * CW, CW, HP * HB])).then_inc(in_x0[slot], 16)

            def ids_to_all(out, fields, rows):
                return sp.dma_start(out, t["ids_half"][fields, rows].unsqueeze(0).to_broadcast(
                    [TP, fields.stop - fields.start, rows.stop - rows.start]))

            sp.dma_start(ids_flat[:], t["ids_t"].rearrange("f (a b) -> (f a) b", b=S * B // P)).then_inc(in_ids_flat, 16)
            sp.dma_start(ids_all[:], t["ids"].rearrange("(t p) f -> p t f", p=P)).then_inc(in_ids, 16)
            sp.dma_start(windows_c, t["windows_c"].bitcast(bf16)).then_inc(in_win, 16)
            sp.wait_ge(ids_stored, 16)
            ids_to_all(ids_b0[:, N_REST:, :], slice(N_REST, len(HOT)), slice(0, CH)).then_inc(in_ids_b0[0], 16)
            ids_to_all(ids_b0[:, 0:N_REST, :], slice(0, N_REST), slice(0, CH)).then_inc(in_ids_b0[1], 16)
            sp.wait_ge(gathered[0], PER_CHUNK[0])
            for unit in range(3):
                load_x0(unit, unit)

            def load_ids(chunk):
                at = (chunk - 1) * CH
                ids_to_all(ids_b[:, :, at:at + CH], slice(0, len(HOT)), slice(at + CH, at + 2 * CH)).then_inc(in_ids_b[chunk - 1], 16)

            load_ids(1)
            sp.dma_start(w1_ctx[:], t["w1_ctx"]).then_inc(in_ctx, 16)
            sp.wait_ge(split, 3)
            sp.wait_ge(m_summed, (FT + 1) // 2)
            for unit in range(3, 5):
                load_x0(unit, unit)

            def reload_x0(i, u):
                sp.wait_ge(z_summed, i * UNITS + u + 1)
                load_x0(i * UNITS + u + X_SLOTS, u % X_SLOTS)

            def store_y(n):
                sp.wait_ge(y_kept, n + 1)
                sp.dma_start(t["out"][bass.ds(n, 1), :], y_row[:]).then_inc(y_stored, 16)

            for u in range(UNITS):
                reload_x0(0, u)
                if u == 0:
                    load_ids(2)
                elif u == 1:
                    sp.dma_start(w1_z[:], t["w1_z"].rearrange("(a p) n -> p a n", p=P)).then_inc(in_tower, 16)
                    sp.dma_start(b_w3[:], t["b_w3"]).then_inc(in_tower, 16)
                    sp.dma_start(w2[:], t["w2"].rearrange("(a p) n -> p a n", p=P)).then_inc(in_tower, 16)
                elif u == 2:
                    sp.wait_ge(ctx_stored, 16 * 3)
                    for part in range(3):
                        at = [n for n in range(8) if STACK_X[n] == part]
                        rows = t["w1_ctx_parts"][part]
                        sp.dma_start(ctx_stack[at[0] * D:(at[-1] + 1) * D, :].rearrange("p (a c) -> p a c", a=CB),
                                     rows[:, :, CW1:].unsqueeze(0).to_broadcast([len(at), D, CB, CX])).then_inc(in_tower, 16)
                    rows = t["w1_ctx_parts"].rearrange("s r a c -> (s r) a c")[:, :, 0:CW1]
                    sp.dma_start(w1_stack[0:6 * D, :].rearrange("p (a c) -> p a c", a=CB),
                                 rows.unsqueeze(0).to_broadcast([2, 3 * D, CB, CW1])).then_inc(in_tower, 16)
                    sp.dma_start(w1_stack[6 * D:, :].rearrange("p (a c) -> p a c", a=CB),
                                 rows[0:2 * D]).then_inc(in_tower, 16)
                    low = t["w1_ctx_parts"][2]
                    sp.dma_start(ctx_low[:].rearrange("p (a c) -> p a c", a=CB), low[:, :, CW1:]).then_inc(in_tower, 16)
                    sp.dma_start(w1_low[:].rearrange("p (a c) -> p a c", a=CB), low[:, :, 0:CW1]).then_inc(in_tower, 16)
                elif u == 3:
                    sp.wait_ge(hot_made, NP)
                    load_ids(3)
            with sp.Fori(1, NCH - 1) as i:
                for u in range(UNITS):
                    reload_x0(i, u)
                    if u % FT == 0:
                        store_y(2 * i - 2 + u // FT)
            for u in range(UNITS - X_SLOTS):
                reload_x0(NCH - 1, u)
                if u == 0:
                    store_y(2 * NCH - 4)
            for n in range(2 * NCH - 3, 2 * NCH):
                store_y(n)
            sp.wait_ge(y_stored, 16 * 2 * NCH)

        @block.gpsimd
        def _(pool):
            def gathers(g):
                for f in NEW[g]:
                    if f not in HOT:
                        for bt in range(BT):
                            nc.gpsimd.indirect_dma_start(
                                out=e[:, bt, f * D:(f + 1) * D], out_offset=None, in_=t[f"tbl_{f}"][:, :],
                                in_offset=bass.IndirectOffsetOnAxis(ap=ids_now[:, bt, f:f + 1], axis=0)
                            ).then_inc(gathered[g], 16)

            pool.wait_ge(in_ids, 16)
            nc.gpsimd.tensor_copy(ids_now[:], ids_all[:, 0:BT, :]).then_inc(ids_copied, 1)
            pool.wait_ge(ids_copied, 1)
            for g in range(FT):
                gathers(g)

            def chunk_gathers(c):
                for g in range(FT):
                    fields = slice(NEW[g][0], NEW[g][-1] + 1)
                    pool.wait_ge(gathered[g], c * PER_CHUNK[g])
                    pool.sem_inc(gathers_begun, 1)
                    nc.gpsimd.tensor_copy(ids_now[:, :, fields], ids_all[:, bass.ds(c * BT, BT), fields]).then_inc(ids_copied, 1)
                    pool.wait_ge(e_spread, (c - 1) * FT + spreads_that_read(g))
                    pool.sem_inc(gathers_begun, 1)
                    pool.wait_ge(ids_copied, (c - 1) * FT + g + 2)
                    pool.sem_inc(gathers_begun, 1)
                    gathers(g)

            chunk_gathers(1)
            with pool.Fori(2, NCH) as c:
                chunk_gathers(c)

        @block.vector
        def _(dve):
            def make_hot(i, first, c, n):
                pair = PAIRS[n]
                if not (first and c == 0 and n < 2):
                    dve.wait_ge(hot_used, (i + c) * NP + n - 1)
                at = HOT.index(pair[0])
                if first and c == 0:
                    dve.wait_ge(ids_rel, 1 if n == 0 else 2)
                    ids = ids_b0[:, at:at + 2, :]
                else:
                    dve.wait_ge(ids_rel, (i + c) + 2)
                    ids = ids_b[:, at:at + 2, bass.ds((i + c - 1) * CH, CH)]
                for k in range(KT[pair[1]]):
                    lo = int(k >= KT[pair[0]])
                    last = nc.vector.tensor_scalar(onehot[:, n % 2, lo:2, k, :], ids[:, lo:2, :], float(k), None, ALU.is_equal)
                last.then_inc(hot_made, 1)

            def keep_rows(i, first, c, n):
                dve.wait_ge(hot_used, (i + c) * NP + n + 1)
                if not (first and c == 0):
                    dve.wait_ge(e_spread, (i + c - 1) * FT + spreads_that_read(group_of(PAIRS[n][1])))
                for half, f in enumerate(PAIRS[n]):
                    parts_ps = o_bank[n % 2][:, half * BT * 3 * D:(half + 1) * BT * 3 * D].rearrange("p (b s d) -> p b d s", b=BT, s=3)
                    last = nc.vector.tensor_reduce(e[:, :, f * D:(f + 1) * D], parts_ps, AX.X, ALU.add)
                last.then_inc(rows_kept, 1)

            dve.wait_ge(in_ids_flat, 16)
            nc.vector.tensor_scalar(ids_half[:], ids_flat[:], 2048.0, None, ALU.min).then_inc(ids_cast, 1)
            nc.vector.memset(e[:, :, S * D:], 0.0).then_inc(padded, 1)
            dve.wait_ge(in_alpha, 16)
            for n in range(3):
                src = alpha[:] if n == 0 else alpha_r[:, n - 1, :, :]
                if n > 0:
                    dve.wait_ge(alpha_rest, n)
                nc.vector.tensor_copy(alpha_p[:, :, n, :], src).then_inc(alpha_split, 1)
                if n < 2:
                    dve.wait_ge(alpha_split, n + 1)
                    nc.vector.tensor_tensor(alpha_r[:, n, :, :], src, alpha_p[:, :, n, :], ALU.subtract).then_inc(alpha_rest, 1)
            dve.wait_ge(in_small, 16 * N_SMALL_LOADS)
            for a in range(2):
                last = nc.vector.tensor_scalar(v_dk[:, a, :], w_hv[:, a, 0:D], w_hv[:, a, D:D + 1], None, ALU.mult)
            last.then_inc(v_made, 1)
            dve.wait_ge(v_made, 1)
            for a in range(2):
                last = nc.vector.tensor_tensor(
                    v_diag[:, a, :].rearrange("p (g k h) -> p g k h", g=HP, k=K),
                    v_dk[:, a, :].rearrange("p (g h) -> p g h", g=HP).unsqueeze(2).to_broadcast([P, HP, K, 2]),
                    k_mask.unsqueeze(1).unsqueeze(3).to_broadcast([P, HP, K, 2]), ALU.mult)
            last.then_inc(v_spread, 1)
            dve.wait_ge(in_table_1, 16 * len(HEAD_TABLES))
            for n in range(3):
                src = table[:, 0:HEAD, :] if n == 0 else rest_1[:, n - 1, :, :]
                if n > 0:
                    dve.wait_ge(rest_1_made, n)
                nc.vector.tensor_copy(parts[:, 0:HEAD, n, :], src).then_inc(split_1, 1)
                if n < 2:
                    dve.wait_ge(split_1, n + 1)
                    nc.vector.tensor_tensor(rest_1[:, n, :, :], src, parts[:, 0:HEAD, n, :], ALU.subtract).then_inc(rest_1_made, 1)
            for ft in range(FT):
                dve.wait_ge(ab_summed, ft + 1)
                nc.vector.tensor_reduce(ab[:, ft, :].rearrange("p (d k) -> p d k", k=K),
                                        ab_bank[ft][:, 0:D // 2 * 3 * K].rearrange("p (d s k) -> p d k s", s=3, k=K),
                                        AX.X, ALU.add).then_inc(ab_kept, 1)
            def make_rest(n):
                dve.wait_ge(split, n + 1)
                if n == 1:
                    dve.wait_ge(rest_made, 1)
                nc.vector.tensor_tensor(rest[n], table[:, HEAD:, :] if n == 0 else rest[0], parts[:, HEAD:, n, :],
                                        ALU.subtract).then_inc(rest_made, 1)

            pending = []

            def keep_pending(i, first, slot):
                while pending and pending[0][0] <= slot:
                    keep_rows(i, first, *pending.pop(0)[1:])

            def make_pairs(i, first, slot):
                for c, n in of_slot(pairs, first, True, slot):
                    make_hot(i, first, c, n)
                    pending.append((slot, c, n))

            def cut_m(n):
                dve.wait_ge(m_summed, n + 1)
                groups = min(2, FT - 2 * n)
                nc.vector.tensor_tensor(m_w[:, 2 * n:2 * n + groups, :],
                                        m_bank[n][:, 0:groups * 2 * P].rearrange("p (a c) -> p a c", a=groups),
                                        h_mask.unsqueeze(1).to_broadcast([P, groups, 2 * P]), ALU.mult).then_inc(m_kept, 1)

            make_rest(0)
            make_hot(0, True, 0, 0)
            make_rest(1)
            keep_rows(0, True, 0, 0)
            cut_m(0)
            make_hot(0, True, 0, 1)
            cut_m(1)
            cut_m(2)
            pending.append((-1, 0, 1))

            def chunk_units(i, first, more):
                for u in range(UNITS):
                    ft = u % FT
                    dve.wait_ge(in_x0[u % X_SLOTS], i * (UNITS // X_SLOTS * 16) + (u // X_SLOTS + 1) * 16)
                    if u < FT:
                        dve.wait_ge(win_kept, i * FT + ft + 1)
                    unit = x0[:, u % X_SLOTS, :].rearrange("p (q b) -> p q b", q=HP)
                    nc.vector.tensor_tensor(
                        unit, unit, e_win[:, ft, u // FT * HB:(u // FT + 1) * HB].unsqueeze(1).to_broadcast([P, HP, HB]),
                        ALU.mult).then_inc(prod_made, 1)
                    if more:
                        if first:
                            keep_pending(i, first, u - 1)
                        if first and u in (1, 2):
                            dve.wait_ge(ctx_split, u)
                            if u == 2:
                                dve.wait_ge(ctx_rest, 1)
                            nc.vector.tensor_tensor(w1_ctx_rest[:, u - 1, :], w1_ctx[:] if u == 1 else w1_ctx_rest[:, 0, :],
                                                    w1_ctx_p[:, u - 1, :], ALU.subtract).then_inc(ctx_rest, 1)
                        make_pairs(i, first, u)
                        if not first:
                            keep_pending(i, first, u - 2)
                assert not pending

            chunk_units(0, True, True)
            with dve.Fori(1, NCH - 1) as i:
                chunk_units(i, False, True)
            chunk_units(NCH - 1, False, False)

        @block.scalar
        def _(act):
            act.dma_start(alpha[:], t["alpha"].rearrange("(g p) k -> p g k", p=P)).then_inc(in_alpha, 16)
            act.wait_ge(ids_cast, 1)
            act.dma_start(t["ids_half"].rearrange("f (a b) -> (f a) b", b=S * B // P), ids_half[:]).then_inc(ids_stored, 16)
            act.dma_start(consts[:], t["consts"]).then_inc(in_small, 16)
            act.dma_start(w_hv[:], t["w_hv"].rearrange("(a p) h -> p a h", p=P)).then_inc(in_small, 16)

            def load_table(f):
                return act.dma_start(table[:, KT_AT[f]:KT_AT[f] + KT[f], :], t[f"tbl_{f}"].rearrange("(p k) d -> p k d", p=TP))

            for f in HEAD_TABLES:
                load_table(f).then_inc(in_table_1, 16)
            for f in TABLES[len(HEAD_TABLES):]:
                load_table(f).then_inc(in_tables, 16)

            def from_first_row(ids, lo, hi, done):
                for m, (a, b, _) in enumerate(SIZES):
                    a, b = max(a, lo), min(b, hi)
                    if a < b:
                        last = nc.scalar.activation(ids[:, a:b, :], ids[:, a:b, :], ACT.Identity,
                                                    bias=consts[0:TP, AT_ROW + m:AT_ROW + m + 1])
                if done:
                    last.then_inc(ids_rel, 1)

            act.wait_ge(in_small, 16 * N_SMALL_LOADS)
            act.wait_ge(in_ids_b0[0], 16)
            from_first_row(ids_b0, N_REST, len(HOT), True)
            act.wait_ge(in_tables, 16 * N_REST)
            nc.scalar.copy(parts[:, HEAD:, 0, :], table[:, HEAD:, :]).then_inc(split, 1)
            for ft in range(FT):
                act.wait_ge(ab_turned, ft + 1)
                src = turned_bank[ft][:, 0:2 * CW * CW].rearrange("p (m c) -> p m c", c=CW)
                nc.scalar.copy(ab_t[:, ft, :, :].rearrange("p s (f h c) -> p (s f) h c", h=2, c=CW),
                               src.unsqueeze(2).to_broadcast([P, 2 * 8, 2, CW])).then_inc(ab_t_kept, 1)
                if ft == 2:
                    act.wait_ge(in_ids_b0[1], 16)
                    from_first_row(ids_b0, 0, N_REST, True)
            for n in range(2):
                act.wait_ge(rest_made, n + 1)
                nc.scalar.copy(parts[:, HEAD:, n + 1, :], rest[n]).then_inc(split, 1)

            def spread_e(i, first, c, ft):
                act.wait_ge(rows_kept, (i + c) * NP + pairs_before(ft))
                act.wait_ge(gathered[ft], (i + (c + 1)) * PER_CHUNK[ft])
                if first and c == 0:
                    act.wait_ge(padded, 1)
                else:
                    act.wait_ge(win_turned, (i + c - 1) * FT + ft + 1)
                base, inner = WINDOWS[ft]
                for lo in range(2):
                    for bt in range(BT):
                        src = bass.AP(e, bt * EC + base + inner * lo, [[BT * EC, P], [13, 4], [0, 2], [1, CW]])
                        dst = bass.AP(e_cols, bt * FT * P + ft * P + 2 * CW * lo,
                                      [[BT * FT * P, P], [4 * CW, 4], [CW, 2], [1, CW]])
                        last = nc.scalar.copy(dst, src)
                last.then_inc(e_spread, 1)

            def keep_windows(i, first, c, ft):
                act.wait_ge(win_turned, (i + c) * FT + ft + 1)
                if not (first and c == 0):
                    act.wait_ge(prod_made, (i + c - 1) * UNITS + FT + ft + 1)
                nc.scalar.copy(e_win[:, ft, :], v_bank[:]).then_inc(win_kept, 1)

            for c, ft in WINS_0[-1]:
                spread_e(0, True, c, ft)
                keep_windows(0, True, c, ft)

            def tower_step(n, step):
                layer, m, k = step
                if k != LAST_INPUT[layer]:
                    return
                if layer == "layer1":
                    act.wait_ge(h1_summed, n * (H1 // P) + m + 1)
                    nc.scalar.activation(h1[:, m, :], w_bank[L1_BANK[m]][:, 0:HB], ACT.Relu, bias=b1[:, m:m + 1]).then_inc(h1_made, 1)
                elif layer == "layer2":
                    act.wait_ge(h2_summed, n * (H2 // P) + m + 1)
                    nc.scalar.activation(h2[:, m, :], w_bank[L2_BANK[m]][:, 0:HB], ACT.Relu, bias=b2[:, m:m + 1]).then_inc(h2_made, 1)
                else:
                    act.wait_ge(y_summed, n + 1)
                    nc.scalar.copy(y_row[:], w_bank[Y_BANK][0:1, 0:HB]).then_inc(y_kept, 1)

            def chunk_rest(i, first, more):
                for u in range(UNITS):
                    half, step = divmod(u, FT)
                    now = 2 * i + half
                    tower = u >= FT or not first
                    if first and u == FT:
                        act.wait_ge(in_tower, 16 * N_TOWER_LOADS)
                    if tower and step == FT - 1:
                        for piece in BEFORE_FIFTH:
                            tower_step(now - 1, piece)
                    for c, ft in of_slot(windows, first, more, u):
                        if (c, ft) in of_slot(spreads, first, more, u):
                            spread_e(i, first, c, ft)
                        keep_windows(i, first, c, ft)
                    if step == FT - 1:
                        act.wait_ge(z_summed, i * UNITS + u + 1)
                        for a in range(2):
                            nc.scalar.copy(z_t[:, a, :], z_bank[a][:, 0:HB]).then_inc(z_kept, 1)
                    if tower:
                        if step == FT - 1 and not (first and half == 1):
                            act.wait_ge(y_stored, (now - 1) * 16)
                        for piece in TOWER_STEPS[step]:
                            tower_step(now - 1, piece)
                    for c, ft in of_slot(spreads, first, more, u):
                        if (c, ft) not in of_slot(windows, first, more, u):
                            spread_e(i, first, c, ft)
                    if first and u < 3:
                        if u == 0:
                            act.wait_ge(in_ctx, 16)
                        else:
                            act.wait_ge(ctx_rest, u)
                        nc.scalar.copy(w1_ctx_p[:, u, :], w1_ctx[:] if u == 0 else w1_ctx_rest[:, u - 1, :]).then_inc(ctx_split, 1)
                    if first and u == 2:
                        act.wait_ge(ctx_split, 3)
                        for part in range(3):
                            act.dma_start(t["w1_ctx_parts"][part].rearrange("r a c -> (r a) c"),
                                          w1_ctx_p[:, part, :]).then_inc(ctx_stored, 16)
                    if first and u == 0:
                        act.wait_ge(in_ids_b[0], 16)
                        from_first_row(ids_b[:, :, 0:CH], 0, len(HOT), True)
                    elif first and u != FT:
                        chunk, lo = (2, 2 * u - 2) if u < FT else (3, 2 * (u - FT) - 2)
                        act.wait_ge(in_ids_b[chunk - 1], 16)
                        from_first_row(ids_b[:, :, (chunk - 1) * CH:chunk * CH], lo, lo + 2, lo + 2 == len(HOT))

            chunk_rest(0, True, True)
            with act.Fori(1, NCH - 1) as i:
                chunk_rest(i, False, True)
            chunk_rest(NCH - 1, False, False)
            act.wait_ge(y_stored, 16 * (2 * NCH - 1))
            for piece in _MATMULS:
                tower_step(2 * NCH - 1, piece)

        @block.tensor
        def _(pe):
            def table_rows(i, first, pairs):
                for c, n in pairs:
                    pe.wait_ge(hot_made, (i + c) * NP + n + 1)
                    if not (first and c == 0 and n < 2):
                        pe.wait_ge(rows_kept, (i + c) * NP + n - 1)
                    for half, f in enumerate(PAIRS[n]):
                        for bt in range(BT):
                            at = (half * BT + bt) * 3 * D
                            for k in range(KT[f]):
                                last = nc.tensor.matmul(o_bank[n % 2][:, at:at + 3 * D],
                                                        onehot[:, n % 2, half, k, bt * P:(bt + 1) * P],
                                                        parts[:, KT_AT[f] + k, :, :].rearrange("p s d -> p (s d)"),
                                                        start=k == 0, stop=k == KT[f] - 1)
                    last.then_inc(hot_used, 1)

            def turn_windows(i, first, wins):
                for c, ft in wins:
                    pe.wait_ge(e_spread, (i + c) * FT + ft + 1)
                    if (first, c, ft) != (True, 0, 0):
                        pe.wait_ge(win_kept, (i + c) * FT + ft)
                    for bt in range(BT):
                        last = nc.tensor.transpose(v_bank[:, bt * P:(bt + 1) * P], e_cols[:, bt, ft * P:(ft + 1) * P], ident)
                    last.then_inc(win_turned, 1)

            pe.wait_ge(alpha_split, 3)
            pe.wait_ge(in_win, 16)
            for ft in range(FT):
                for d in range(D // 2):
                    last = nc.tensor.matmul(ab_bank[ft][:, d * 3 * K:(d + 1) * 3 * K], windows_c[:, ft, d, :],
                                            alpha_p[:, ft, :, :].rearrange("p s k -> p (s k)"), start=True, stop=True)
                last.then_inc(ab_summed, 1)
            pe.wait_ge(in_small, 16 * N_SMALL_LOADS)
            for ft in range(FT):
                pe.wait_ge(ab_kept, ft + 1)
                nc.tensor.transpose(turned_bank[ft][:, 0:P], ab[:, ft, :], ident).then_inc(ab_turned, 1)
            pe.wait_ge(v_spread, 1)

            def sum_m(n):
                for ft in range(2 * n, min(2 * n + 2, FT)):
                    pe.wait_ge(ab_t_kept, min(ft + 2, FT))
                    at = ft % 2 * 2 * P
                    for a in range(2):
                        last = nc.tensor.matmul(m_bank[n][:, at:at + 2 * P], ab_t[:, ft, a, :], v_diag[:, a, :],
                                                start=a == 0, stop=a == 1)
                last.then_inc(m_summed, 1)

            sum_m(0)
            pe.wait_ge(split_1, 3)
            table_rows(0, True, PAIRS_0[-1][:1])
            sum_m(1)
            sum_m(2)
            turn_windows(0, True, WINS_0[-1])
            pe.wait_ge(split, 3)
            table_rows(0, True, PAIRS_0[-1][1:])
            pe.wait_ge(m_kept, (FT + 1) // 2)

            def contract(i, first, u):
                half, ft = divmod(u, FT)
                pe.wait_ge(prod_made, i * UNITS + u + 1)
                for hp in range(HP):
                    a, q = divmod(hp, QH)
                    if ft == 0 and q == 0 and not (first and half == 0):
                        pe.wait_ge(z_kept, (2 * i + half - 1) * 2 + a + 1)
                    last = nc.tensor.matmul(z_bank[a][q * ZW:(q + 1) * ZW, 0:HB], m_w[:, ft, hp * ZW:(hp + 1) * ZW],
                                            x0[:, u % X_SLOTS, hp * HB:(hp + 1) * HB], start=ft == 0, stop=ft == FT - 1)
                last.then_inc(z_summed, 1)

            def tower_step(n, step, first=False):
                layer, m, k = step
                if layer == "layer1":
                    if (m, k) == (0, 0):
                        pe.wait_ge(z_kept, 2 * n + 2)
                    if (m, k) == (0, 1) and not first:
                        pe.wait_ge(y_kept, n)
                    if (m, k) == (2, 1):
                        pe.wait_ge(h1_made, n * (H1 // P) + 1)
                    if k < 2:
                        w, x = w1_z[:, k, m * P:(m + 1) * P], z_t[:, k, :]
                    elif k == 2:
                        w, x = w1_stack[:, m * P:(m + 1) * P], ctx_stack[:, bass.ds(n * HB, HB)]
                    else:
                        w, x = w1_low[:, m * P:(m + 1) * P], ctx_low[:, bass.ds(n * HB, HB)]
                    out, summed = w_bank[L1_BANK[m]][:, 0:HB], h1_summed
                elif layer == "layer2":
                    if m == 0:
                        pe.wait_ge(h1_made, n * (H1 // P) + max(k + 1, 2))
                    out, w, x, summed = w_bank[L2_BANK[m]][:, 0:HB], w2[:, k, m * P:(m + 1) * P], h1[:, k, :], h2_summed
                else:
                    pe.wait_ge(h2_made, n * (H2 // P) + k + 1)
                    out, w, x, summed = w_bank[Y_BANK][0:1, 0:HB], w3[:, k:k + 1], h2[:, k, :], y_summed
                done = k == LAST_INPUT[layer]
                last = nc.tensor.matmul(out, w, x, start=k == FIRST_INPUT[layer], stop=done)
                if done:
                    last.then_inc(summed, 1)

            def chunk_all(i, first, more):
                for u in range(UNITS):
                    half, step = divmod(u, FT)
                    tower = u >= FT or not first
                    if first and u == FT:
                        pe.wait_ge(in_tower, 16 * N_TOWER_LOADS)
                    if tower and step == FT - 1:
                        for piece in BEFORE_FIFTH:
                            tower_step(2 * i + half - 1, piece, first=first)
                    contract(i, first, u)
                    turn_windows(i, first, of_slot(windows, first, more, u))
                    table_rows(i, first, of_slot(pairs, first, more, u))
                    if tower:
                        for piece in TOWER_STEPS[step]:
                            tower_step(2 * i + half - 1, piece, first=first)

            chunk_all(0, True, True)
            with pe.Fori(1, NCH - 1) as i:
                chunk_all(i, False, True)
            chunk_all(NCH - 1, False, False)
            for piece in _MATMULS:
                tower_step(2 * NCH - 1, piece)


def _constants():
    import numpy as np
    part = np.arange(P)
    windows_c = np.zeros((P, FT, D // 2, 2, 8, CW), np.uint16)
    for f in range(F):
        for g in range(256):
            j, d = divmod(g, D)
            windows_c[(f % 8) * 16 + j, f // 8, d // 2, d % 2, f % 8, (256 * f + g) // F - window_start(f)] = 0x3F80
    h_mask = ((part[:, None] // CW) % 2 == np.arange(2 * P)[None, :] % 2).astype(np.float32)
    k_mask = (part[:, None] % K == np.arange(K)[None, :]).astype(np.float32)
    first_row = -part[:, None] * np.array([size for _, _, size in SIZES], np.float32)
    return {"windows_c": windows_c.reshape(P, FT, D // 2, P), 
            "consts": np.concatenate([np.eye(P, dtype=np.float32), h_mask, k_mask, first_row], axis=1, dtype=np.float32)}


def kernel(**inputs):
    import numpy as np
    import concourse.bacc as bacc
    from concourse.bass_utils import run_bass_kernel_spmd

    a = {name: np.asarray(value) for name, value in inputs.items()}
    w1 = a["W_top1"]
    x0 = np.concatenate([a["r_x0"], np.zeros((B, 8 * FT - F, D), np.float32)], axis=1)
    x0 = x0.reshape(2 * NCH, HB, FT, 8, HP, 2).transpose(0, 2, 3, 5, 4, 1)
    arrays = _constants()
    arrays.update({f"tbl_{f}": a[f"tbl_{f}"] for f in range(S)})
    arrays.update({
        "ids": a["ids"], "ids_t": a["ids"].T[HOT + [f for f in range(S) if f not in HOT]],
        "x0": x0.reshape(NCH * UNITS * 2 * CW, HP * HB),
        "alpha": np.concatenate([a["L0_rec_alpha"], np.zeros((P * FT - S * F, K), np.float32)]),
        "w_hv": np.concatenate([a["L0_rec_w"].transpose(2, 0, 1), a["L0_rec_hv"].transpose(1, 0, 2)], axis=2)
                .reshape(D // 2, 2, K, D + 1).transpose(1, 0, 2, 3).reshape(D * K, D + 1),
        "w1_z": w1[0:K * D].reshape(K, HP, 2, H1).transpose(1, 0, 2, 3).reshape(K * D, H1),
        "w1_ctx": np.concatenate([w1[K * D:].reshape(P, CW1), a["dense_ctx"].T.reshape(P, CX)], axis=1), "w2": a["W_top2"],
        "b_w3": np.concatenate([a["b_top1"].reshape(H1 // P, P), a["b_top2"].reshape(H2 // P, P),
                                a["W_top3"].reshape(H2 // P, P)]).T,
    })
    arrays = {f"{name}_dram": np.ascontiguousarray(value) for name, value in arrays.items()}

    nc = bacc.Bacc("TRN2", target_bir_lowering=False, num_devices=1)
    t = {name.removesuffix("_dram"): nc.dram_tensor(name, value.shape, mybir.dt.from_np(value.dtype), kind="ExternalInput").ap()
         for name, value in arrays.items()}
    t["ids_half"] = nc.dram_tensor("ids_half_dram", (S, B), mybir.dt.float16).ap()
    t["w1_ctx_parts"] = nc.dram_tensor("w1_ctx_parts_dram", (3, D, CB, CW1 + CX), mybir.dt.bfloat16).ap()
    out = nc.dram_tensor("out_dram", (B, 1), mybir.dt.float32, kind="ExternalOutput").ap()
    t["out"] = out.rearrange("(c b) o -> c (b o)", c=2 * NCH)
    program(nc, t)
    return run_bass_kernel_spmd(nc, [arrays], core_ids=[0]).results[0]["out_dram"]
```
